# Optimizing a Trainium2 kernel written in Bass

```python
import numpy as np
import jax
import jax.numpy as jnp

def _softmax(x, axis=-1):
    return jax.nn.softmax(x, axis=axis)

def _gelu(x):
    return jax.nn.gelu(x, approximate=True)

def _silu(x):
    return jax.nn.silu(x)

def _sigmoid(x):
    return jax.nn.sigmoid(x)

def _layernorm(x, axis=-1, eps=1e-05):
    m = jnp.mean(x, axis=axis, keepdims=True)
    v = jnp.var(x, axis=axis, keepdims=True)
    return (x - m) / jnp.sqrt(v + eps)

def _scatter_add(tgt, idx, src, axis=0):
    return tgt.at[idx].add(src)

def _segment_sum(src, seg, n):
    return jax.ops.segment_sum(src, seg, n)
kernel_name = 'mk_gnn_preln_d2_gnn_r32_376f50'

def setup_inputs(seed: int=0):
    np.random.seed(seed)
    _w = jnp.asarray

    def _rec_inputs():
        import jax
        import jax.numpy as jnp
        _gk = jax.random.key(seed)
        x = -0.0002653 + 1 * jax.random.normal(jax.random.fold_in(_gk, 1), (50000, 128), jnp.float32)
        src = jax.random.randint(jax.random.fold_in(_gk, 2), (25000,), 0, 50000, jnp.int32)
        dst = jax.random.randint(jax.random.fold_in(_gk, 3), (25000,), 0, 50000, jnp.int32)
        _o = jnp.argsort(dst, stable=True)
        src = src[_o]
        dst = dst[_o]
        edge_attr_64 = 0.000189758 + 1.00013 * jax.random.normal(jax.random.fold_in(_gk, 12), (25000, 64), jnp.float32)
        return (x, src, dst, edge_attr_64)
    x, src, dst, edge_attr_64 = _rec_inputs()

    def _L0_gnn_setup():
        import jax, jax.numpy as jnp
        import numpy as np
        N, E, D_IN, H, D = (170000, 37500, 128, 4, 32)
        NEG_SLOPE = 0.2
        key = jax.random.key(seed)
        ks = jax.random.split(key, 8)
        x = jax.random.normal(ks[0], (N, D_IN), dtype=jnp.float32)
        W_embed = jax.random.normal(ks[1], (D_IN, H * D), dtype=jnp.float32) * (2.0 / (D_IN + H * D)) ** 0.5
        a_src = jax.random.normal(ks[2], (H, D), dtype=jnp.float32) * (2.0 / (1 + H * D)) ** 0.5
        a_dst = jax.random.normal(ks[3], (H, D), dtype=jnp.float32) * (2.0 / (1 + H * D)) ** 0.5
        W_lin = jax.random.normal(ks[4], (D_IN, H * D), dtype=jnp.float32) * (2.0 / (D_IN + H * D)) ** 0.5
        bias = jnp.zeros((H * D,), dtype=jnp.float32)
        src = jax.random.randint(ks[5], (E,), 0, N, dtype=jnp.int32)
        dst = jax.random.randint(ks[6], (E,), 0, N, dtype=jnp.int32)
        return {'x': x, 'W_embed': W_embed, 'a_src': a_src, 'a_dst': a_dst, 'W_lin': W_lin, 'bias': bias, 'src': src, 'dst': dst}
    _L0_gnn_all = _L0_gnn_setup()
    _L0_gnn_in = {k: v for k, v in _L0_gnn_all.items() if k in ('W_embed', 'a_src', 'a_dst', 'W_lin', 'bias')}
    del _L0_gnn_all

    def _L1_gnn_setup():
        import jax, jax.numpy as jnp
        import numpy as np
        N = 50000
        E = 25000
        D = 128
        BOND = 64
        key = jax.random.key(seed)
        ks = jax.random.split(key, 8)
        h = jax.random.normal(ks[0], (N, D), dtype=jnp.float32)
        edge_index = jax.random.randint(ks[1], (2, E), 0, N, dtype=jnp.int64)
        bond_emb = jax.random.normal(ks[2], (E, BOND), dtype=jnp.float32)
        lim1 = 1.0 / np.sqrt(2 * D + BOND)
        W1 = jax.random.uniform(ks[3], (2 * D + BOND, D), minval=-lim1, maxval=lim1, dtype=jnp.float32)
        b1 = jnp.zeros((D,), dtype=jnp.float32)
        lim2 = 1.0 / np.sqrt(D)
        W2 = jax.random.uniform(ks[4], (D, D), minval=-lim2, maxval=lim2, dtype=jnp.float32)
        b2 = jnp.zeros((D,), dtype=jnp.float32)
        lim3 = 1.0 / np.sqrt(BOND)
        Wa = jax.random.uniform(ks[5], (BOND, 1), minval=-lim3, maxval=lim3, dtype=jnp.float32)
        ba = jnp.zeros((1,), dtype=jnp.float32)
        return {'h': h, 'edge_index': edge_index, 'bond_emb': bond_emb, 'W1': W1, 'b1': b1, 'W2': W2, 'b2': b2, 'Wa': Wa, 'ba': ba}
    _L1_gnn_all = _L1_gnn_setup()
    _L1_gnn_in = {k: v for k, v in _L1_gnn_all.items() if k in ('W1', 'b1', 'W2', 'b2', 'Wa', 'ba')}
    del _L1_gnn_all
    return {'x': x, 'src': src, 'dst': dst, 'edge_attr_64': edge_attr_64, 'L0_gnn_W_embed': _L0_gnn_in['W_embed'], 'L0_gnn_a_src': _L0_gnn_in['a_src'], 'L0_gnn_a_dst': _L0_gnn_in['a_dst'], 'L0_gnn_W_lin': _L0_gnn_in['W_lin'], 'L0_gnn_bias': _L0_gnn_in['bias'], 'L1_gnn_W1': _L1_gnn_in['W1'], 'L1_gnn_b1': _L1_gnn_in['b1'], 'L1_gnn_W2': _L1_gnn_in['W2'], 'L1_gnn_b2': _L1_gnn_in['b2'], 'L1_gnn_Wa': _L1_gnn_in['Wa'], 'L1_gnn_ba': _L1_gnn_in['ba']}

def reference(x, src, dst, edge_attr_64, L0_gnn_W_embed, L0_gnn_a_src, L0_gnn_a_dst, L0_gnn_W_lin, L0_gnn_bias, L1_gnn_W1, L1_gnn_b1, L1_gnn_W2, L1_gnn_b2, L1_gnn_Wa, L1_gnn_ba):
    import jax
    import jax.numpy as jnp

    def _L0_gnn_ref(x, W_embed, a_src, a_dst, W_lin, bias, src, dst):
        import jax, jax.numpy as jnp
        import numpy as np
        N, E, D_IN, H, D = (170000, 37500, 128, 4, 32)
        NEG_SLOPE = 0.2
        n = x.shape[0]
        h = (x @ W_embed).reshape(n, H, D)
        dot_src = jnp.einsum('nhd,hd->nh', h, a_src)
        dot_dst = jnp.einsum('nhd,hd->nh', h, a_dst)
        z = dot_src[src] + dot_dst[dst]
        logit = jnp.where(z >= 0, z, NEG_SLOPE * z)
        m = jax.ops.segment_max(logit, dst, num_segments=n)
        e = jnp.exp(logit - m[dst])
        denom = jax.ops.segment_sum(e, dst, num_segments=n)
        prob = e / denom[dst]
        msg = h[src] * prob[:, :, None]
        out = jax.ops.segment_sum(msg, dst, num_segments=n)
        out = out.reshape(n, H * D)
        out = out + x @ W_lin
        out = out + bias[None, :]
        return out

    def _L1_gnn_ref(h, edge_index, bond_emb, W1, b1, W2, b2, Wa, ba):
        import jax, jax.numpy as jnp
        import numpy as np
        N = 50000
        E = 25000
        D = 128
        BOND = 64
        row, col = (edge_index[0], edge_index[1])
        bond_weights = jax.nn.sigmoid(bond_emb @ Wa + ba)
        messages = jnp.concatenate([h[row], h[col], bond_emb], axis=-1)
        messages = jax.nn.relu(messages @ W1 + b1) @ W2 + b2
        messages = messages * bond_weights
        h_new = jax.ops.segment_sum(messages, row, num_segments=h.shape[0])
        return h + h_new
    edge_index = jnp.stack([src, dst])
    h = jnp.maximum(_layernorm(x, axis=-1), 0.0)
    x = x + _L0_gnn_ref(h, L0_gnn_W_embed, L0_gnn_a_src, L0_gnn_a_dst, L0_gnn_W_lin, L0_gnn_bias, src, dst)
    h = jnp.maximum(_layernorm(x, axis=-1), 0.0)
    x = x + _L1_gnn_ref(h, edge_index, edge_attr_64, L1_gnn_W1, L1_gnn_b1, L1_gnn_W2, L1_gnn_b2, L1_gnn_Wa, L1_gnn_ba)
    return x

_drawn_inputs = setup_inputs


def setup_inputs(seed=0):
    import zlib

    import numpy as np

    out = dict(_drawn_inputs(seed))
    spreads = {'L0_gnn_bias': (0.0, 0.1), 'L1_gnn_b1': (0.0, 0.8), 'L1_gnn_b2': (0.0, 0.297)}
    factors = {'L0_gnn_a_src': 2.843, 'L0_gnn_a_dst': 8.0, 'L1_gnn_Wa': 4.585}
    for name, (base, spread) in spreads.items():
        noise = np.random.default_rng([zlib.crc32(name.encode()), seed]).standard_normal(out[name].shape)
        drawn = base * np.exp(spread * noise) if base else spread * noise
        out[name] = jnp.asarray(drawn.astype(out[name].dtype))
    for name, factor in factors.items():
        out[name] = (out[name] * factor).astype(out[name].dtype)
    return out
```

```python
from contextlib import ExitStack

import concourse.bass as bass
from concourse import mybir

F32 = mybir.dt.float32
BF16 = mybir.dt.bfloat16
I32 = mybir.dt.int32
ALU = mybir.AluOpType
ACT = mybir.ActivationFunctionType
AX_X = mybir.AxisListType.X

P = 128
D = 128
HEADS = 4
HD = D // HEADS
COLS_PER_IT = 4
ROWS = 8
NODES_PER_IT = P * ROWS
SLOPE = 0.2
EPS = 1e-5
BIG = 3.0e38


def gnn_program(nc, x, src, dst, bond, w_embed, a_src, a_dst, w_lin, bias0, w1, b1, w2, b2, wa, ba, out):
    N = x.shape[0]
    E = src.shape[0]
    BOND = bond.shape[1]
    COLS = -(-E // P)
    COLS += -COLS % COLS_PER_IT
    ITS = COLS // COLS_PER_IT
    FULL = E // COLS
    TAIL = E - FULL * COLS
    LAST = FULL
    assert FULL == P - 1 and 0 < TAIL < COLS and ITS % 2 == 1
    assert ITS == -(-N // NODES_PER_IT)
    PAD = N + P - 1

    def node0(it):
        return N - NODES_PER_IT if isinstance(it, int) and it == ITS - 1 else NODES_PER_IT * it

    def past(k):
        return not isinstance(k, int) or k > 0

    x1 = nc.dram_tensor("x1_rows", (N, D), F32, kind="Internal").ap()
    spill = nc.dram_tensor("base_rows", (P, COLS * D), F32, kind="Internal").ap()

    ctx = ExitStack()
    with ctx:
        def sb(name, shape, dt=F32):
            return ctx.enter_context(nc.sbuf_tensor(name, shape, dt))

        def sem(name):
            return ctx.enter_context(nc.semaphore(name))

        ps = [ctx.enter_context(nc.psum_tensor(f"bank{i}", [P, 512], F32)) for i in range(8)]

        H = sb("H", [P, COLS * D])
        BD = sb("BD", [P, COLS * BOND])
        XE = sb("XE", [P, 2, COLS_PER_IT, 2, D])
        XN = sb("XN", [P, 2, ROWS, D])
        R = sb("R", [P, 16, D])
        TS = sb("TS", [P, 2, 512])
        O = sb("O", [P, 2, ROWS, D])
        BS = sb("BS", [P, 2, COLS_PER_IT, D])
        key0i = sb("key0i", [P, COLS], I32)
        key1i = sb("key1i", [P, COLS], I32)
        nexti = sb("nexti", [P, 1], I32)
        gidx = sb("gidx", [P, COLS, 2], I32)
        sidx = sb("sidx", [P, COLS], I32)
        key0 = sb("key0", [P, COLS])
        key1 = sb("key1", [P, COLS])
        nextf = sb("nextf", [P, 1])
        same = sb("same", [P, COLS])
        nsame = sb("nsame", [P, COLS])
        hmask = sb("hmask", [P, COLS])
        bw = sb("bw", [P, COLS])
        Z = sb("Z", [P, COLS, HEADS])
        ix = sb("ix", [P, 2, COLS_PER_IT, 2], I32)
        sx = sb("sx", [P, 2, COLS_PER_IT], I32)
        ident = sb("ident", [P, P])
        ltri = sb("ltri", [P, P])
        utri = sb("utri", [P, P])
        ones = R[:, 10, :]
        epsc = sb("epsc", [P, 1])
        spare = sb("spare", [P, 1])
        wes = sb("wes", [P, D + HEADS])
        wad = sb("wad", [P, HEADS])
        wl = sb("wl", [P, D])
        w1s = sb("w1s", [P, 3, D])
        w2s = sb("w2s", [P, D])
        abr = R[:, 8:10, :]
        wabr = sb("wabr", [P, BOND])
        babr = sb("babr", [P, 1])
        b1c = sb("b1c", [P, 1])
        brow = TS[0:1, 0, 0:2 * D].rearrange("p (n d) -> p n d", n=2)
        b3 = sb("b3", [1, 2, 3, D], BF16)
        bt = TS[0:1, 1, 0:2 * D].rearrange("p (n d) -> p n d", n=2)
        on1 = sb("on1", [1, P], BF16)
        st = sb("st", [P, 16, 6])
        sa = sb("sa", [P, 2, 16])
        sm = sb("sm", [P, 16])
        sc = sb("sc", [P, 16])
        var = sb("var", [P, 2, 16])
        std = sb("std", [P, 2, 16])
        rstd = sb("rstd", [P, 2, 16])
        nmr = sb("nmr", [P, 2, 16])

        def col(j):
            return bass.ds(j * D, D)

        ld_idx, ld_w, ld_bd = sem("ld_idx"), sem("ld_w"), sem("ld_bd")
        pads_set, tri_init, consts, zeroed, wchain, idx_done = (sem(n) for n in (
            "pads_set", "tri_init", "consts", "zeroed", "wchain", "idx_done"))
        dummy_rows = sem("dummy_rows")
        with nc.Block() as block:
            @block.sync
            def _(sp):
                sp.wait_ge(pads_set, 4)
                for t, a in ((key0i, dst), (key1i, src)):
                    sp.dma_start(t[0:FULL, :], a[0:FULL * COLS].rearrange("(p j) -> p j", j=COLS)).then_inc(ld_idx, 16)
                    sp.dma_start(t[LAST:P, 0:TAIL], a[FULL * COLS:E].rearrange("(p j) -> p j", p=1)).then_inc(ld_idx, 16)
                with nc.allow_non_contiguous_dma(reason="one key per partition"):
                    sp.dma_start(nexti[0:FULL - 1, :],
                                 dst[COLS:FULL * COLS].rearrange("(p j) -> p j", j=COLS)[:, 0:1]).then_inc(ld_idx, 16)
                    sp.dma_start(nexti[FULL - 1:FULL, :],
                                 dst[FULL * COLS:FULL * COLS + 1].rearrange("(p j) -> p j", p=1)).then_inc(ld_idx, 16)
                sp.dma_start(BD[0:112, :], bond[0:112 * COLS, :].rearrange("(p j) c -> p (j c)", j=COLS)).then_inc(ld_bd, 16)
                sp.dma_start(BD[112:FULL, :], bond[112 * COLS:FULL * COLS, :].rearrange("(p j) c -> p (j c)", j=COLS)).then_inc(ld_bd, 16)
                sp.dma_start(BD[LAST:P, 0:TAIL * BOND], bond[FULL * COLS:E, :].rearrange("(p j) c -> p (j c)", p=1)).then_inc(ld_bd, 16)
                sp.wait_ge(zeroed, 1)
                sp.dma_start(out[N:N + P, :], O[:, 0, 0, :]).then_inc(dummy_rows, 16)
                sp.wait_ge(dummy_rows, 16)

            @block.scalar
            def _(act):
                act.dma_start(wes[:, 0:D], w_embed).then_inc(ld_w, 16)
                act.dma_start(wl[:, :], w_lin).then_inc(ld_w, 16)
                act.dma_start(abr[:, 0, :], a_src.rearrange("(o h) d -> o (h d)", o=1).to_broadcast([P, D])).then_inc(ld_w, 16)
                act.dma_start(abr[:, 1, :], a_dst.rearrange("(o h) d -> o (h d)", o=1).to_broadcast([P, D])).then_inc(ld_w, 16)
                act.dma_start(w1s[:, 0, :], w1[0:D, :]).then_inc(ld_w, 16)
                act.dma_start(w1s[:, 1, :], w1[D:2 * D, :]).then_inc(ld_w, 16)
                act.dma_start(w1s[0:BOND, 2, :], w1[2 * D:2 * D + BOND, :]).then_inc(ld_w, 16)
                act.dma_start(w2s[:, :], w2).then_inc(ld_w, 16)
                act.dma_start(wabr[:, :], wa.rearrange("c o -> o c").to_broadcast([P, BOND])).then_inc(ld_w, 16)
                act.dma_start(babr[:, :], ba.rearrange("(o c) -> o c", o=1).to_broadcast([P, 1])).then_inc(ld_w, 16)
                with nc.allow_non_contiguous_dma(reason="a bias per partition"):
                    act.dma_start(b1c[:, :], b1.rearrange("(p o) -> p o", o=1)).then_inc(ld_w, 16)
                act.dma_start(brow[:, 0, :], bias0.rearrange("(o c) -> o c", o=1)).then_inc(ld_w, 16)
                act.dma_start(brow[:, 1, :], b2.rearrange("(o c) -> o c", o=1)).then_inc(ld_w, 16)

            @block.gpsimd
            def _(pool):
                nc.gpsimd.memset(ones, 1.0).then_inc(tri_init, 1)
                pool.wait_ge(tri_init, 1)
                for t, pattern, mult, op in ((ident, [[-1, P]], 1, ALU.is_equal), (ltri, [[-1, P]], 1, ALU.is_gt),
                                             (utri, [[1, P]], -1, ALU.is_gt)):
                    nc.gpsimd.affine_select(out=t[:, :], in_=ones, compare_op=op, fill=0.0, base=0,
                                            pattern=pattern, channel_multiplier=mult).then_inc(consts, 1)
                nc.gpsimd.iota(spare[:, :], [[0, 1]], base=N, channel_multiplier=1,
                               allow_small_or_imprecise_dtypes=True).then_inc(consts, 1)

            @block.vector
            def _(dve):
                links = [0]

                def link(ins):
                    links[0] += 1
                    ins.then_inc(wchain, 1)
                    dve.wait_ge(wchain, links[0])

                nc.vector.memset(key0i[:, :], PAD).then_inc(pads_set, 1)
                nc.vector.memset(key1i[:, :], PAD).then_inc(pads_set, 1)
                nc.vector.memset(nexti[:, :], PAD).then_inc(pads_set, 1)
                nc.vector.memset(BD[96:P, :], 0.0).then_inc(pads_set, 1)
                nc.vector.memset(O[:, 0, 0, :], 0.0).then_inc(zeroed, 1)
                nc.vector.memset(epsc[:, :], EPS)
                nc.vector.memset(on1[:, :], 1.0)
                nc.vector.memset(same[:, :], 0.0)
                link(nc.vector.memset(nsame[:, :], 0.0))
                dve.wait_ge(ld_w, 16 * 13)
                for k, res in ((0, wes[:, D:D + HEADS]), (1, wad[:, :])):
                    link(nc.vector.tensor_tensor(R[:, k, :], wes[:, 0:D], abr[:, k, :], ALU.mult))
                    link(nc.vector.tensor_reduce(res, R[:, k, :].rearrange("p (h d) -> p h d", h=HEADS), AX_X, ALU.add))
                link(nc.vector.tensor_copy(b3[:, :, 0, :], brow[:, :, :]))
                link(nc.vector.tensor_tensor(bt[:, :, :], brow[:, :, :], b3[:, :, 0, :], ALU.subtract))
                link(nc.vector.tensor_copy(b3[:, :, 1, :], bt[:, :, :]))
                link(nc.vector.tensor_tensor(bt[:, :, :], bt[:, :, :], b3[:, :, 1, :], ALU.subtract))
                link(nc.vector.tensor_copy(b3[:, :, 2, :], bt[:, :, :]))
                dve.wait_ge(ld_idx, 16 * 6)
                nc.vector.tensor_copy(key0[:, :], key0i[:, :])
                nc.vector.tensor_copy(key1[:, :], key1i[:, :])
                link(nc.vector.tensor_copy(nextf[:, :], nexti[:, :]))
                nc.vector.tensor_scalar(gidx[:, :, 0], key1[:, :], float(N - 1), None, ALU.min)
                nc.vector.tensor_scalar(gidx[:, :, 1], key0[:, :], float(N - 1), None, ALU.min)
                nc.vector.tensor_scalar(hmask[:, :], key0[:, :], key0[:, 0:1], None, ALU.is_equal)
                link(nc.vector.tensor_tensor(same[:, 1:COLS], key0[:, 1:COLS], key0[:, 0:COLS - 1], ALU.is_equal))
                link(nc.vector.tensor_copy(nsame[:, 0:COLS - 1], same[:, 1:COLS]))
                far = float(2 ** 20)
                nc.vector.tensor_copy(R[:, 0:1, 0:COLS - D], nsame[:, D:COLS].rearrange("p (o c) -> p o c", o=1))
                link(nc.vector.tensor_copy(R[:, 4, 0:D], nsame[:, 0:D]))
                link(nc.vector.tensor_scalar(R[:, 0, COLS - D - 1:COLS - D], key0[:, COLS - 1:COLS], nextf[:, 0:1], None, ALU.is_equal))
                nc.vector.scalar_tensor_tensor(sidx[:, D:COLS], R[:, 0, 0:COLS - D], far, key0[:, D:COLS], ALU.mult, ALU.add)
                nc.vector.scalar_tensor_tensor(sidx[:, 0:D], R[:, 4, 0:D], far, key0[:, 0:D], ALU.mult, ALU.add).then_inc(idx_done, 1)
                dve.wait_ge(idx_done, 1)
                dve.wait_ge(ld_bd, 16 * 3)
                dve.wait_ge(consts, 4)

        def stats(tile_ap, t):
            return nc.vector.bn_stats(st[:, t, :], tile_ap)

        def moments(link, par, n, done):
            link(nc.vector.tensor_tensor(sm[:, 0:n], st[:, 0:n, 1], st[:, 0:n, 4], ALU.subtract))
            nc.vector.tensor_tensor(sa[:, par, 0:n], st[:, 0:n, 1], st[:, 0:n, 4], ALU.add)
            nc.vector.tensor_tensor(sc[:, 0:n], st[:, 0:n, 2], st[:, 0:n, 5], ALU.add)
            link(nc.vector.tensor_tensor(sm[:, 0:n], sm[:, 0:n], sm[:, 0:n], ALU.mult))
            nc.vector.scalar_tensor_tensor(var[:, par, 0:n], sm[:, 0:n], D / 4.0, sc[:, 0:n], ALU.mult, ALU.add).then_inc(done, 1)

        def scales(link, par, n, done):
            link(nc.vector.reciprocal(rstd[:, par, 0:n], std[:, par, 0:n]))
            nc.vector.scalar_tensor_tensor(nmr[:, par, 0:n], sa[:, par, 0:n], -0.5, rstd[:, par, 0:n],
                                           ALU.mult, ALU.mult).then_inc(done, 1)

        def root(par, n, done):
            nc.scalar.activation(std[:, par, 0:n], var[:, par, 0:n], ACT.Sqrt, bias=epsc[:, 0:1], scale=1.0 / D).then_inc(done, 1)

        def normalise(dst_ap, src_ap, par, t):
            return nc.scalar.activation(dst_ap, src_ap, ACT.Relu, bias=nmr[:, par, t:t + 1], scale=rstd[:, par, t:t + 1])

        def loop(eng, body):
            body(0, 0, 0)
            body(1, 1, 0)
            with eng.Fori(1, ITS // 2) as i:
                body(2 * i, 0, i)
                body(2 * i + 1, 1, i)
            body(ITS - 1, 0, ITS // 2)

        ld_xe = [sem("l0_gathered0"), sem("l0_gathered1")]
        ld_xn = [sem("l0_nodes0"), sem("l0_nodes1")]
        var_ready, std_ready, norm_ready, r_ready = (sem(n) for n in ("l0_var", "l0_std", "l0_norm", "l0_rows"))
        t_ready, ts_even, ts_odd, mm_done, h_taken, out_taken, h_go = (sem(n) for n in (
            "l0_transposed", "l0_ts_even", "l0_ts_odd", "l0_products", "l0_h_taken", "l0_out_taken", "l0_h_go"))
        st_o = [sem("l0_stored0"), sem("l0_stored1")]
        st_b = [sem("l0_spilled0"), sem("l0_spilled1")]
        vchain, ix_ready, go = sem("l0_vchain"), sem("l0_ix"), sem("l0_go")
        psT, psA, psB = ps[0:2], ps[2:4], ps[4:6]
        G4 = COLS_PER_IT
        with nc.Block() as block:
            @block.gpsimd
            def _(pool):
                lim = pool.to_reg(N - 1)

                def body(it, u, k):
                    if past(k):
                        pool.wait_ge(out_taken, G4 * (it - 1))
                        pool.wait_ge(r_ready, G4 * (it - 1))
                    nc.gpsimd.tensor_copy(ix[:, u, :, :], gidx[:, bass.ds(it * G4, G4), :]).then_inc(ix_ready, 1)
                    pool.wait_ge(ix_ready, it + 1)
                    pool.sem_inc(go, 1)
                    for c in range(G4):
                        for s in range(2):
                            pool.indirect_dma_start(XE[:, u, c, s, :], None, x, bass.IndirectOffsetOnAxis(ix[:, u, c, s:s + 1], 0),
                                                    bounds_check=lim, oob_is_err=False).then_inc(ld_xe[u], 16)
                loop(pool, body)

            @block.sync
            def _(sp):
                def load(it, u, k):
                    if past(k):
                        sp.wait_ge(out_taken, G4 * (it - 1))
                        sp.wait_ge(r_ready, G4 * (it - 1))
                    sp.dma_start(XN[:, u, :, :], x[bass.ds(node0(it), NODES_PER_IT), :].rearrange("(p r) c -> p r c", r=ROWS)
                                 ).then_inc(ld_xn[u], 16)

                def store(it, u, k):
                    sp.wait_ge(out_taken, G4 * (it + 1))
                    if isinstance(it, int) and it == ITS - 1:
                        sp.wait_ge(st_o[1], 16 * (ITS // 2))
                    sp.dma_start(x1[bass.ds(node0(it), NODES_PER_IT), :].rearrange("(p r) c -> p r c", r=ROWS),
                                 O[:, u, :, :]).then_inc(st_o[u], 16)
                    sp.dma_start(spill[:, bass.ds(it * G4 * D, G4 * D)],
                                 BS[:, u, :, :].rearrange("p c d -> p (c d)")).then_inc(st_b[u], 16)

                load(0, 0, 0)
                load(1, 1, 0)
                store(0, 0, 0)
                with sp.Fori(1, ITS // 2) as i:
                    load(2 * i, 0, i)
                    store(2 * i - 1, 1, i)
                    load(2 * i + 1, 1, i)
                    store(2 * i, 0, i)
                load(ITS - 1, 0, ITS // 2)
                store(ITS - 2, 1, ITS // 2)
                store(ITS - 1, 0, ITS // 2)
                for u in range(2):
                    sp.wait_ge(st_o[u], 16 * (ITS // 2 + 1 - u))
                    sp.wait_ge(st_b[u], 16 * (ITS // 2 + 1 - u))

            @block.vector
            def _(dve):
                LINKS = 3

                def tile_stats(it, u, k, g, link):
                    if g == 0:
                        dve.wait_ge(ld_xe[u], 16 * 2 * G4 * (k + 1))
                        dve.wait_ge(ld_xn[u], 16 * (k + 1))
                    for s in range(2):
                        stats(XE[:, u, g, s, :], 4 * g + s)
                    stats(XN[:, u, 2 * g, :], 4 * g + 2)
                    last = stats(XN[:, u, 2 * g + 1, :], 4 * g + 3)
                    if g == G4 - 1:
                        link(last)
                        moments(link, u, 16, var_ready)

                def linker(base):
                    n = [0]

                    def link(ins):
                        n[0] += 1
                        ins.then_inc(vchain, 1)
                        dve.wait_ge(vchain, base + n[0])
                    return link

                LINKS = 4

                def take(it, u, k, g):
                    j = it * G4 + g
                    dve.wait_ge(mm_done, G4 * it + g + 1)
                    nc.vector.tensor_tensor(BS[:, u, g, :], psB[g % 2][:, 2 * D:3 * D], XE[:, u, g, 1, :], ALU.add)
                    nc.vector.tensor_copy(Z[:, bass.ds(j, 1), :], psB[g % 2][:, 3 * D:3 * D + HEADS].rearrange("p (o h) -> p o h", o=1))
                    nc.vector.tensor_tensor(O[:, u, 2 * g:2 * g + 2, :], psB[g % 2][:, 0:2 * D].rearrange("p (r c) -> p r c", r=2),
                                            XN[:, u, 2 * g:2 * g + 2, :], ALU.add).then_inc(out_taken, 1)

                def body(it, u, k):
                    last = isinstance(it, int) and it == ITS - 1
                    link = linker(it * LINKS + 3)
                    dve.wait_ge(std_ready, it + 1)
                    scales(link, u, 16, norm_ready)
                    for g in range(G4):
                        if not last:
                            tile_stats(it + 1, 1 - u, k + u, g, link)
                        if g % 2 == 1:
                            dve.wait_ge(t_ready, G4 * it + g + 1)
                            if not (not past(k) and u == 0 and g < 2):
                                dve.wait_ge(mm_done, G4 * it + g - 1)
                            nc.vector.tensor_copy(TS[:, 1, :], psT[1][:, :]).then_inc(ts_odd, 1)
                        if g == 0 and past(k):
                            dve.wait_ge(st_o[u], 16 * k)
                            dve.wait_ge(st_b[u], 16 * k)
                        if g > 0:
                            take(it, u, k, g - 1)
                    take(it, u, k, G4 - 1)

                first = linker(0)
                for g in range(G4):
                    tile_stats(0, 0, 0, g, first)
                loop(dve, body)

            @block.scalar
            def _(act):
                def take_h(it, g):
                    act.wait_ge(mm_done, G4 * it + g + 1)
                    act.sem_inc(h_go, 1)
                    nc.scalar.copy(H[:, col(it * G4 + g)], psA[g % 2][:, 0:D]).then_inc(h_taken, 1)

                def body(it, u, k):
                    act.wait_ge(norm_ready, it + 1)
                    for g in range(G4 + 1):
                        if g < G4:
                            if not (not past(k) and u == 0):
                                act.wait_ge(t_ready, G4 * (it - 1) + g + 1)
                            for s in range(2):
                                normalise(R[:, 4 * g + s, :], XE[:, u, g, s, :], u, 4 * g + s)
                            normalise(R[:, 4 * g + 2, :], XN[:, u, 2 * g, :], u, 4 * g + 2)
                            normalise(R[:, 4 * g + 3, :], XN[:, u, 2 * g + 1, :], u, 4 * g + 3).then_inc(r_ready, 1)
                        if g > 0:
                            if g % 2 == 1:
                                act.wait_ge(t_ready, G4 * it + g)
                                if not (not past(k) and u == 0 and g < 3):
                                    act.wait_ge(mm_done, G4 * it + g - 2)
                                nc.scalar.copy(TS[:, 0, :], psT[0][:, :]).then_inc(ts_even, 1)
                        if g > 1:
                            take_h(it, g - 2)
                    take_h(it, G4 - 1)
                    if not (isinstance(it, int) and it == ITS - 1):
                        act.wait_ge(var_ready, it + 2)
                        root(1 - u, 16, std_ready)

                act.wait_ge(var_ready, 1)
                root(0, 16, std_ready)
                loop(act, body)

            @block.tensor
            def _(pe):
                def product(it, first, g):
                    a, b, t = psA[g % 2], psB[g % 2], TS[:, g % 2, :]
                    pe.wait_ge((ts_even, ts_odd)[g % 2], 2 * it + g // 2 + 1)
                    if not (first and g < 2):
                        pe.wait_ge(out_taken, G4 * it + g - 1)
                        pe.wait_ge(h_taken, G4 * it + g - 1)
                    nc.tensor.matmul(a[:, 0:D], t[:, 0:D], wes[:, 0:D], start=True, stop=True, skip_group_check=True)
                    z = b[:, 3 * D:3 * D + HEADS]
                    nc.tensor.matmul(z, t[:, 0:D], wes[:, D:D + HEADS], start=True, stop=False, skip_group_check=True)
                    nc.tensor.matmul(z, t[:, D:2 * D], wad[:, :], start=False, stop=True, skip_group_check=True)
                    base = b[:, 2 * D:3 * D]
                    for n in range(3):
                        nc.tensor.matmul(base, on1[:, :], b3[:, 0, n, :], start=(n == 0), stop=False, skip_group_check=True)
                    nc.tensor.matmul(base, t[:, D:2 * D], wl[:, :], start=False, stop=True, skip_group_check=True)
                    for r in range(2):
                        o = b[:, r * D:(r + 1) * D]
                        for n in range(3):
                            nc.tensor.matmul(o, on1[:, :], b3[:, 0, n, :], start=(n == 0), stop=False, skip_group_check=True)
                        last = nc.tensor.matmul(o, t[:, (2 + r) * D:(3 + r) * D], wl[:, :], start=False, stop=True, skip_group_check=True)
                    last.then_inc(mm_done, 1)

                def body(it, u, k):
                    first = not past(k) and u == 0
                    for g in range(G4):
                        pe.wait_ge(r_ready, G4 * it + g + 1)
                        if not (first and g < 2):
                            pe.wait_ge((ts_even, ts_odd)[g % 2], 2 * it + g // 2)
                        for q in range(4):
                            last = nc.tensor.transpose(psT[g % 2][:, q * D:(q + 1) * D], R[:, 4 * g + q, :], ident[:, :])
                        last.then_inc(t_ready, 1)
                        if g > 0:
                            product(it, first, g - 1)
                    product(it, first, G4 - 1)
                loop(pe, body)

        def view(t, n, m):
            return t.rearrange("p (a b) -> p a b", b=m) if n else t
        Rf = R[:, :, :].rearrange("p t d -> p (t d)")
        Of = O[:, :, :, :].rearrange("p u r d -> p (u r d)")
        Xf = XE[:, :, :, :, :].rearrange("p u c s d -> p (u c s d)")
        Nf = XN[:, :, :, :].rearrange("p u r d -> p (u r d)")
        CH = COLS * HEADS
        F = Rf[:, 0:CH].rearrange("p (j h) -> p j h", h=HEADS)
        Q = Rf[:, CH:2 * CH].rearrange("p (j h) -> p j h", h=HEADS)
        M = Of[:, 0:CH].rearrange("p (j h) -> p j h", h=HEADS)
        pen = Of[:, CH:CH + COLS]
        penn = Of[:, CH + COLS:CH + 2 * COLS]
        tmask = Of[:, CH + 2 * COLS:CH + 3 * COLS]
        free_ = Of[:, CH + 3 * COLS:CH + 4 * COLS]
        rows = Xf[:, 0:10 * 256].rearrange("p (a q) -> p a q", q=256) if False else None
        keyr = Xf[:, 0:256]
        valr = Xf[:, 256:256 + HEADS * 256].rearrange("p (h q) -> p h q", q=256)
        m_h = Xf[:, 1280:1536]
        m_t = Xf[:, 1536:1792]
        work = Nf[:, 0:HEADS * 256].rearrange("p (h q) -> p h q", q=256)
        pm = Nf[:, 1024:1280]
        ends = Nf[:, 1280:1296]
        tot = Nf[:, 1296:1304].rearrange("p (s h) -> p s h", h=HEADS)
        carry_mask = Nf[:, 1408:1536]
        carry = Nf[:, 1536:1664]
        bwork = TS[:, :, :].rearrange("p u c -> p (u c)")
        zb = Of[:, CH + 4 * COLS:CH + 5 * COLS]
        BCH = 14
        s_v, s_ready, s_pe, s_exp, s_bw, s_sig, s_p4 = (sem(n) for n in (
            "sm_chain", "sm_ends", "sm_rows", "sm_exp", "sm_bond", "sm_sigmoid", "sm_run"))
        s_c = sem("sm_carry")
        with nc.Block() as block:
            @block.tensor
            def _(pe):
                for r in range(3):
                    pe.wait_ge(s_ready, r + 1)
                    n = 2 if r == 0 else 2 * HEADS
                    for q in range(n):
                        c = (key0[:, 0:1], key0[:, COLS - 1:COLS])[q] if r == 0 else ends[:, q:q + 1]
                        last = nc.tensor.transpose(ps[3 * (r % 2) + q // 4][:, (q % 4) * P:(q % 4 + 1) * P],
                                                   c.to_broadcast([P, P]), ident[:, :])
                    last.then_inc(s_pe, 1)
                pe.wait_ge(s_ready, 4)
                nc.tensor.matmul(ps[6][:, 0:D], carry_mask, H[:, (COLS - 1) * D:COLS * D], start=True, stop=True).then_inc(s_c, 1)

            @block.scalar
            def _(act):
                act.wait_ge(s_exp, 1)
                nc.scalar.activation(Z[:, :, :], Z[:, :, :], ACT.Exp).then_inc(s_exp, 1)
                act.wait_ge(s_bw, 1)
                nc.scalar.activation(bw[:, :], zb, ACT.Sigmoid, bias=babr[:, 0:1]).then_inc(s_sig, 1)

            @block.vector
            def _(dve):
                links = [0]

                def link(ins):
                    links[0] += 1
                    ins.then_inc(s_v, 1)
                    dve.wait_ge(s_v, links[0])

                nc.vector.tensor_copy(pen[:, 0:1], key0[:, 0:1]).then_inc(s_ready, 1)
                for h in range(HEADS):
                    link(nc.vector.tensor_scalar(F[:, :, h], Z[:, :, h], SLOPE, None, ALU.mult))
                link(nc.vector.tensor_tensor(Z[:, :, :], Z[:, :, :], F[:, :, :], ALU.max))
                link(nc.vector.tensor_scalar(pen, same[:, :], -1.0, BIG, ALU.add, ALU.mult))
                nc.vector.tensor_scalar(penn, nsame[:, :], -1.0, BIG, ALU.add, ALU.mult)
                link(nc.vector.tensor_scalar(tmask, key0[:, :], key0[:, COLS - 1:COLS], None, ALU.is_equal))
                link(nc.vector.tensor_tensor(free_, hmask[:, :], tmask, ALU.max))
                link(nc.vector.tensor_scalar(free_, free_, -1.0, 1.0, ALU.mult, ALU.add))
                link(nc.vector.scalar_tensor_tensor(tmask, hmask[:, :], -1.0, tmask, ALU.mult, ALU.add))
                link(nc.vector.tensor_scalar(tmask, tmask, 0.0, None, ALU.max))

                for h in range(HEADS):
                    link(nc.vector.tensor_tensor_scan(F[:, :, h], pen, Z[:, :, h], -BIG, ALU.add, ALU.max))
                for h in range(HEADS):
                    link(nc.vector.tensor_tensor_scan(Q[:, ::-1, h], penn[:, ::-1], F[:, ::-1, h], 0.0, ALU.add, ALU.max))
                link(nc.vector.tensor_copy(ends[:, 0:HEADS], Q[:, 0, :]))
                dve.wait_ge(s_pe, 1)
                link(nc.vector.tensor_copy(keyr, ps[0][:, 0:256]))
                link(nc.vector.tensor_scalar(m_h, keyr, key0[:, 0:1], None, ALU.is_equal))
                link(nc.vector.tensor_scalar(m_t, keyr, key0[:, COLS - 1:COLS], None, ALU.is_equal))
                nc.vector.tensor_copy(ends[:, HEADS:2 * HEADS], Q[:, COLS - 1, :]).then_inc(s_ready, 1)

                def combine(bank0, r, is_max):
                    dve.wait_ge(s_pe, r)
                    for half in range(2):
                        link(nc.vector.tensor_copy(valr[:, :, half * P:(half + 1) * P],
                                                   ps[bank0 + half][:, :].rearrange("p (h q) -> p h q", q=P)))
                    for s, m in ((0, m_h), (1, m_t)):
                        for h in range(HEADS):
                            link(nc.vector.tensor_tensor(work[:, h, :], valr[:, h, :], m, ALU.mult))
                        if is_max:
                            link(nc.vector.tensor_scalar(pm, m, -1.0, BIG, ALU.add, ALU.mult))
                            for h in range(HEADS):
                                link(nc.vector.tensor_tensor(work[:, h, :], work[:, h, :], pm, ALU.add))
                        link(nc.vector.tensor_reduce(tot[:, s, :], work[:, :, :], AX_X, ALU.max if is_max else ALU.add))
                    for h in range(HEADS):
                        link(nc.vector.tensor_tensor(M[:, :, h], Q[:, :, h], free_, ALU.mult))
                        link(nc.vector.scalar_tensor_tensor(M[:, :, h], hmask[:, :], tot[:, 0, h:h + 1], M[:, :, h], ALU.mult, ALU.add))
                        link(nc.vector.scalar_tensor_tensor(M[:, :, h], tmask, tot[:, 1, h:h + 1], M[:, :, h], ALU.mult, ALU.add))

                combine(3, 2, True)
                nc.vector.tensor_tensor(Z[:, :, :], Z[:, :, :], M[:, :, :], ALU.subtract).then_inc(s_exp, 1)
                dve.wait_ge(s_exp, 2)
                for h in range(HEADS):
                    link(nc.vector.tensor_tensor_scan(F[:, :, h], same[:, :], Z[:, :, h], 0.0, ALU.mult, ALU.add))
                link(nc.vector.tensor_scalar(pen, nsame[:, :], -1.0, 1.0, ALU.mult, ALU.add))
                for h in range(HEADS):
                    link(nc.vector.tensor_tensor(F[:, :, h], F[:, :, h], pen, ALU.mult))
                for h in range(HEADS):
                    link(nc.vector.tensor_tensor_scan(Q[:, ::-1, h], nsame[:, ::-1], F[:, ::-1, h], 0.0, ALU.mult, ALU.add))
                link(nc.vector.tensor_copy(ends[:, 0:HEADS], Q[:, 0, :]))
                link(nc.vector.tensor_scalar(pm[:, 0:1], hmask[:, COLS - 1:COLS], -1.0, 1.0, ALU.mult, ALU.add))
                nc.vector.tensor_scalar(ends[:, HEADS:2 * HEADS], Q[:, COLS - 1, :], pm[:, 0:1], None, ALU.mult).then_inc(s_ready, 1)
                combine(0, 3, False)
                link(nc.vector.reciprocal(M[:, :, :], M[:, :, :]))
                link(nc.vector.tensor_tensor(Z[:, :, :], Z[:, :, :], M[:, :, :], ALU.mult))

                for b in range(COLS // BCH):
                    w = bwork[:, 0:BCH * BOND].rearrange("p (j c) -> p j c", c=BOND)
                    link(nc.vector.tensor_tensor(w, BD[:, b * BCH * BOND:(b + 1) * BCH * BOND].rearrange("p (j c) -> p j c", c=BOND),
                                                 wabr[:, :].unsqueeze(1).to_broadcast([P, BCH, BOND]), ALU.mult))
                    link(nc.vector.tensor_reduce(zb[:, b * BCH:(b + 1) * BCH], w, AX_X, ALU.add))
                nc.vector.tensor_copy(pm[:, 0:1], zb[:, 0:1]).then_inc(s_bw, 1)

                def run(it, base, first):
                    n = [0]

                    def step(ins):
                        n[0] += 1
                        ins.then_inc(s_p4, 1)
                        dve.wait_ge(s_p4, base + n[0])
                    hv = H[:, bass.ds(it * G4 * D, G4 * D)].rearrange("p (g d) -> p g d", d=HD)
                    pv = Z[:, bass.ds(it * G4, G4), :].rearrange("p j h -> p (j h)").unsqueeze(2).to_broadcast([P, G4 * HEADS, HD])
                    step(nc.vector.tensor_tensor(hv, hv, pv, ALU.mult))
                    for c in range(G4):
                        if first and c == 0:
                            continue
                        j = it * G4 + c
                        step(nc.vector.scalar_tensor_tensor(H[:, col(j)], H[:, col(j - 1)], same[:, bass.ds(j, 1)], H[:, col(j)],
                                                            ALU.mult, ALU.add))
                run(0, 0, True)
                with dve.Fori(1, ITS) as i:
                    run(i, 5 * i - 1, False)
                link(nc.vector.scalar_tensor_tensor(carry_mask, keyr[:, 0:P], key0[:, COLS - 1:COLS], utri[:, :], ALU.is_equal, ALU.mult))
                nc.vector.tensor_copy(pm[:, 0:1], keyr[:, 0:1]).then_inc(s_ready, 1)
                dve.wait_ge(s_c, 1)
                link(nc.vector.tensor_copy(carry, ps[6][:, 0:D]))
                dve.wait_ge(s_sig, 1)

        ld_b = [sem("sc_base0"), sem("sc_base1")]
        sc_done = [sem("sc_done0"), sem("sc_done1")]
        sc_rows, sc_chain, sc_ix, sc_go = (sem(n) for n in ("sc_rows", "sc_chain", "sc_ix", "sc_go"))
        W4 = XE[:, :, :, 0, :]
        with nc.Block() as block:
            @block.sync
            def _(sp):
                def body(it, u, k):
                    if past(k):
                        sp.wait_ge(sc_rows, it - 1)
                    sp.dma_start(BS[:, u, :, :].rearrange("p c d -> p (c d)"), spill[:, bass.ds(it * G4 * D, G4 * D)]).then_inc(ld_b[u], 16)
                loop(sp, body)

            @block.vector
            def _(dve):
                def body(it, u, k):
                    if past(k):
                        dve.wait_ge(sc_done[u], 16 * G4 * k)
                    for c in range(G4):
                        j = it * G4 + c
                        last = nc.vector.scalar_tensor_tensor(O[:, u, c, :], carry, hmask[:, bass.ds(j, 1)], H[:, col(j)],
                                                              ALU.mult, ALU.add)
                    last.then_inc(sc_chain, 1)
                    dve.wait_ge(sc_chain, it + 1)
                    dve.wait_ge(ld_b[u], 16 * (k + 1))
                    nc.vector.tensor_tensor(O[:, u, 0:G4, :], O[:, u, 0:G4, :], BS[:, u, :, :], ALU.add).then_inc(sc_rows, 1)
                loop(dve, body)

            @block.gpsimd
            def _(pool):
                lim = pool.to_reg(N - 1)

                def body(it, u, k):
                    if past(k):
                        pool.wait_ge(sc_done[u], 16 * G4 * k)
                    nc.gpsimd.tensor_copy(sx[:, u, :], sidx[:, bass.ds(it * G4, G4)]).then_inc(sc_ix, 1)
                    pool.wait_ge(sc_ix, it + 1)
                    pool.wait_ge(sc_rows, it + 1)
                    pool.sem_inc(sc_go, 1)
                    for c in range(G4):
                        pool.indirect_dma_start(x1, bass.IndirectOffsetOnAxis(sx[:, u, c:c + 1], 0), O[:, u, c, :], None,
                                                bounds_check=lim, oob_is_err=False).then_inc(sc_done[u], 16)
                loop(pool, body)
                for u in range(2):
                    pool.wait_ge(sc_done[u], 16 * G4 * (ITS // 2 + 1 - u))

        dn_ld = [sem("dn_nodes0"), sem("dn_nodes1")]
        dn_st = [sem("dn_stored0"), sem("dn_stored1")]
        dn_var, dn_std, dn_norm, dn_r, dn_o, dn_chain = (sem(n) for n in ("dn_var", "dn_std", "dn_norm", "dn_rows", "dn_out", "dn_chain"))
        with nc.Block() as block:
            @block.sync
            def _(sp):
                def load(it, u, k):
                    if past(k):
                        sp.wait_ge(dn_o, it - 1)
                    sp.dma_start(XN[:, u, :, :], x1[bass.ds(node0(it), NODES_PER_IT), :].rearrange("(p r) c -> p r c", r=ROWS)
                                 ).then_inc(dn_ld[u], 16)

                def store(it, u, k):
                    sp.wait_ge(dn_o, it + 1)
                    if isinstance(it, int) and it == ITS - 1:
                        sp.wait_ge(dn_st[1], 16 * (ITS // 2))
                    sp.dma_start(out[bass.ds(node0(it), NODES_PER_IT), :].rearrange("(p r) c -> p r c", r=ROWS),
                                 O[:, u, :, :]).then_inc(dn_st[u], 16)
                load(0, 0, 0)
                load(1, 1, 0)
                store(0, 0, 0)
                with sp.Fori(1, ITS // 2) as i:
                    load(2 * i, 0, i)
                    store(2 * i - 1, 1, i)
                    load(2 * i + 1, 1, i)
                    store(2 * i, 0, i)
                load(ITS - 1, 0, ITS // 2)
                store(ITS - 2, 1, ITS // 2)
                store(ITS - 1, 0, ITS // 2)
                for u in range(2):
                    sp.wait_ge(dn_st[u], 16 * (ITS // 2 + 1 - u))

            @block.vector
            def _(dve):
                def linker(base):
                    n = [0]

                    def link(ins):
                        n[0] += 1
                        ins.then_inc(dn_chain, 1)
                        dve.wait_ge(dn_chain, base + n[0])
                    return link

                def measure(it, u, k, link):
                    dve.wait_ge(dn_ld[u], 16 * (k + 1))
                    for r in range(ROWS):
                        last = stats(XN[:, u, r, :], r)
                    link(last)
                    moments(link, u, ROWS, dn_var)

                def body(it, u, k):
                    link = linker(4 * it + 3)
                    dve.wait_ge(dn_std, it + 1)
                    scales(link, u, ROWS, dn_norm)
                    if not (isinstance(it, int) and it == ITS - 1):
                        measure(it + 1, 1 - u, k + u, link)
                    if past(k):
                        dve.wait_ge(dn_st[u], 16 * k)
                    dve.wait_ge(dn_r, it + 1)
                    nc.vector.tensor_tensor(O[:, u, :, :], XN[:, u, :, :], R[:, bass.ds(ROWS * u, ROWS), :], ALU.add).then_inc(dn_o, 1)
                measure(0, 0, 0, linker(0))
                loop(dve, body)

            @block.scalar
            def _(act):
                def body(it, u, k):
                    act.wait_ge(dn_norm, it + 1)
                    if past(k):
                        act.wait_ge(dn_o, it - 1)
                    for r in range(ROWS):
                        last = normalise(R[:, ROWS * u + r, :], XN[:, u, r, :], u, r)
                    last.then_inc(dn_r, 1)
                    if not (isinstance(it, int) and it == ITS - 1):
                        act.wait_ge(dn_var, it + 2)
                        root(1 - u, ROWS, dn_std)
                act.wait_ge(dn_var, 1)
                root(0, ROWS, dn_std)
                loop(act, body)

        def h_part(n):
            return H[:, n * 512:(n + 1) * 512]
        HS, HDt, BT, HID, S, MS = (h_part(n) for n in range(6))
        UPD = [h_part(6), h_part(7)]
        RR = H[:, 4096:5120].rearrange("p (t d) -> p t d", d=D)
        junk = H[:, 5632:6144]
        cnt = H[:, 5248:5252]
        tt = H[:, 5252:5256]
        kcol = H[:, 5256:5260]
        bnd = H[:, 5264:5264 + G4 * BOND]
        ld_g = [sem("ms_gathered0"), sem("ms_gathered1")]
        (ms_var, ms_std, ms_norm, ms_src, ms_dst, ms_kb, ms_ts, ms_td, ms_hs, ms_hd, ms_bt, ms_s, ms_hid, ms_hidr, ms_msg,
         ms_scaled, ms_sum, ms_upd, ms_ix, ms_go, ms_sgo, ms_sx, ms_add, ms_chain, ms_col) = (sem("ms_" + n) for n in (
            "var", "std", "norm", "src", "dst", "kb", "ts", "td", "hs", "hd", "bt", "s", "hid", "hidr", "msg",
            "scaled", "sum", "upd", "ix", "go", "sgo", "sx", "add", "chain", "col"))
        bK, bB, bS, bD, bH, bM, bU = ps[0:7]
        with nc.Block() as block:
            @block.gpsimd
            def _(pool):
                lim = pool.to_reg(N - 1)
                limo = pool.to_reg(N + P - 1)

                def fetch_ix(it, u, k):
                    if past(k):
                        pool.wait_ge(ms_dst, it - 1)
                    nc.gpsimd.tensor_copy(ix[:, u, :, :], gidx[:, bass.ds(it * G4, G4), :]).then_inc(ms_ix, 1)
                    pool.wait_ge(ms_ix, it + 1)
                    pool.sem_inc(ms_go, 1)

                def fetch(u, c):
                    for s in range(2):
                        pool.indirect_dma_start(XE[:, u, c, s, :], None, x1, bass.IndirectOffsetOnAxis(ix[:, u, c, s:s + 1], 0),
                                                bounds_check=lim, oob_is_err=False).then_inc(ld_g[u], 16)

                def body(it, u, k):
                    more = not (isinstance(it, int) and it >= ITS - 2)
                    if more:
                        fetch_ix(it + 2, u, k + 1)
                    for c in range(G4):
                        if more:
                            fetch(u, c)
                        if c == 0:
                            pool.wait_ge(ms_sx, it + 1)
                            pool.wait_ge(ms_upd, it + 1)
                        if not (not past(k) and u == 0 and c == 0):
                            pool.wait_ge(ms_add, 16 * (G4 * it + c))
                        pool.sem_inc(ms_sgo, 1)
                        pool.indirect_dma_start(out, bass.IndirectOffsetOnAxis(sx[:, u, c:c + 1], 0), UPD[u][:, c * D:(c + 1) * D], None,
                                                bounds_check=limo, oob_is_err=True, compute_op=ALU.add).then_inc(ms_add, 16)
                for n in range(2):
                    fetch_ix(n, n, 0)
                    for c in range(G4):
                        fetch(n, c)
                body(0, 0, 0)
                body(1, 1, 0)
                with pool.Fori(1, ITS // 2 - 1) as i:
                    body(2 * i, 0, i)
                    body(2 * i + 1, 1, i)
                for it in range(ITS - 3, ITS):
                    body(it, it % 2, it // 2)
                pool.wait_ge(ms_add, 16 * COLS)

            @block.vector
            def _(dve):
                LINKS = 7

                def linker(base):
                    n = [0]

                    def link(ins):
                        n[0] += 1
                        ins.then_inc(ms_chain, 1)
                        dve.wait_ge(ms_chain, base + n[0])
                    return link

                def measure(it, u, k, link):
                    dve.wait_ge(ld_g[u], 16 * 2 * G4 * (k + 1))
                    for s in range(2):
                        for c in range(G4):
                            last = stats(XE[:, u, c, s, :], G4 * s + c)
                    link(last)
                    moments(link, u, 2 * G4, ms_var)

                def body(it, u, k):
                    first = not past(k) and u == 0
                    link = linker(LINKS * it + 3)
                    dve.wait_ge(ms_std, it + 1)
                    scales(link, u, 2 * G4, ms_norm)
                    dve.wait_ge(ms_kb, it + 1)
                    if not first:
                        dve.wait_ge(ms_sum, it)
                    for c in range(G4):
                        kc = key1[:, bass.ds(it * G4 + c, 1)]
                        nc.vector.tensor_scalar(S[:, c * D:(c + 1) * D], bK[:, c * D:(c + 1) * D], kc, None, ALU.is_equal)
                        last = nc.vector.scalar_tensor_tensor(junk[:, c * D:(c + 1) * D], bK[:, c * D:(c + 1) * D], kc, ltri[:, :], ALU.is_equal, ALU.mult,
                                                              accum_out=cnt[:, c:c + 1])
                    nc.vector.tensor_copy(BT[0:BOND, :], bB[0:BOND, :]).then_inc(ms_bt, 1)
                    dve.wait_ge(ms_bt, it + 1)
                    link(nc.vector.tensor_scalar(tt, cnt, 1.0, None, ALU.min))
                    k4 = key1[:, bass.ds(it * G4, G4)]
                    link(nc.vector.tensor_scalar(cnt, k4, -1.0, spare[:, 0:1], ALU.mult, ALU.add))
                    link(nc.vector.tensor_tensor(cnt, cnt, tt, ALU.mult))
                    if past(k):
                        dve.wait_ge(ms_add, 16 * G4 * (it - 1))
                    nc.vector.tensor_tensor(sx[:, u, :], cnt, k4, ALU.add).then_inc(ms_sx, 1)
                    if not (isinstance(it, int) and it == ITS - 1):
                        measure(it + 1, 1 - u, k + u, link)
                    dve.wait_ge(ms_msg, it + 1)
                    for c in range(G4):
                        last = nc.vector.tensor_scalar(MS[:, c * D:(c + 1) * D], bM[:, c * D:(c + 1) * D], bw[:, bass.ds(it * G4 + c, 1)],
                                                       None, ALU.mult)
                    last.then_inc(ms_scaled, 1)
                measure(0, 0, 0, linker(0))
                loop(dve, body)

            @block.scalar
            def _(act):
                def columns(it):
                    nc.scalar.copy(bnd, BD[:, bass.ds(it * G4 * BOND, G4 * BOND)])
                    nc.scalar.copy(kcol, key1[:, bass.ds(it * G4, G4)]).then_inc(ms_col, 1)

                def body(it, u, k):
                    first = not past(k) and u == 0
                    act.wait_ge(ms_norm, it + 1)
                    if not first:
                        act.wait_ge(ms_td, it)
                    for s, done in ((0, ms_src), (1, ms_dst)):
                        for c in range(G4):
                            last = normalise(RR[:, G4 * s + c, :], XE[:, u, c, s, :], u, G4 * s + c)
                        last.then_inc(done, 1)
                    if not first:
                        act.wait_ge(ms_hid, it)
                    act.wait_ge(ms_ts, it + 1)
                    nc.scalar.copy(HS, bS[:, :]).then_inc(ms_hs, 1)
                    act.wait_ge(ms_td, it + 1)
                    nc.scalar.copy(HDt, bD[:, :]).then_inc(ms_hd, 1)
                    act.wait_ge(ms_hid, it + 1)
                    if not first:
                        act.wait_ge(ms_msg, it)
                    nc.scalar.activation(HID, bH[:, :], ACT.Relu, bias=b1c[:, 0:1]).then_inc(ms_hidr, 1)
                    if not (isinstance(it, int) and it == ITS - 1):
                        act.wait_ge(ms_var, it + 2)
                        root(1 - u, 2 * G4, ms_std)
                    act.wait_ge(ms_sum, it + 1)
                    if past(k):
                        act.wait_ge(ms_add, 16 * G4 * (it - 1))
                    nc.scalar.copy(UPD[u], bU[:, :]).then_inc(ms_upd, 1)
                    if not (isinstance(it, int) and it == ITS - 1):
                        columns(it + 1)
                columns(0)
                act.wait_ge(ms_var, 1)
                root(0, 2 * G4, ms_std)
                loop(act, body)

            @block.tensor
            def _(pe):
                def body(it, u, k):
                    first = not past(k) and u == 0
                    if not first:
                        pe.wait_ge(ms_sx, it)
                        pe.wait_ge(ms_bt, it)
                    pe.wait_ge(ms_col, it + 1)
                    for c in range(G4):
                        nc.tensor.transpose(bK[:, c * D:(c + 1) * D], kcol[:, c:c + 1].to_broadcast([P, P]), ident[:, :])
                    for c in range(G4):
                        last = nc.tensor.transpose(bB[0:BOND, c * D:(c + 1) * D], bnd[:, c * BOND:(c + 1) * BOND], ident[:, :])
                    last.then_inc(ms_kb, 1)
                    pe.wait_ge(ms_src, it + 1)
                    if not first:
                        pe.wait_ge(ms_hs, it)
                    for c in range(G4):
                        last = nc.tensor.transpose(bS[:, c * D:(c + 1) * D], RR[:, c, :], ident[:, :])
                    last.then_inc(ms_ts, 1)
                    pe.wait_ge(ms_dst, it + 1)
                    if not first:
                        pe.wait_ge(ms_hd, it)
                    for c in range(G4):
                        last = nc.tensor.transpose(bD[:, c * D:(c + 1) * D], RR[:, G4 + c, :], ident[:, :])
                    last.then_inc(ms_td, 1)
                    pe.wait_ge(ms_bt, it + 1)
                    if not first:
                        pe.wait_ge(ms_hidr, it)
                    nc.tensor.matmul(bH[:, :], w1s[0:BOND, 2, :], BT[0:BOND, :], start=True, stop=False)
                    pe.wait_ge(ms_hs, it + 1)
                    nc.tensor.matmul(bH[:, :], w1s[:, 0, :], HS, start=False, stop=False)
                    pe.wait_ge(ms_hd, it + 1)
                    nc.tensor.matmul(bH[:, :], w1s[:, 1, :], HDt, start=False, stop=True).then_inc(ms_hid, 1)
                    pe.wait_ge(ms_hidr, it + 1)
                    if not first:
                        pe.wait_ge(ms_scaled, it)
                    for c in range(G4):
                        o = bM[:, c * D:(c + 1) * D]
                        for n in range(3):
                            nc.tensor.matmul(o, on1[:, :], b3[:, 1, n, :], start=(n == 0), stop=False, skip_group_check=True)
                        last = nc.tensor.matmul(o, HID[:, c * D:(c + 1) * D], w2s[:, :], start=False, stop=True, skip_group_check=True)
                    last.then_inc(ms_msg, 1)
                    pe.wait_ge(ms_scaled, it + 1)
                    if not first:
                        pe.wait_ge(ms_upd, it)
                    for c in range(G4):
                        last = nc.tensor.matmul(bU[:, c * D:(c + 1) * D], S[:, c * D:(c + 1) * D], MS[:, c * D:(c + 1) * D],
                                                start=True, stop=True, skip_group_check=True)
                    last.then_inc(ms_sum, 1)
                loop(pe, body)


_INS = ['x', 'src', 'dst', 'edge_attr_64', 'L0_gnn_W_embed', 'L0_gnn_a_src', 'L0_gnn_a_dst', 'L0_gnn_W_lin', 'L0_gnn_bias',
        'L1_gnn_W1', 'L1_gnn_b1', 'L1_gnn_W2', 'L1_gnn_b2', 'L1_gnn_Wa', 'L1_gnn_ba']


def kernel(**inputs):
    import numpy as _np
    import concourse.bacc as _bacc
    from concourse import mybir as _mybir
    from concourse.bass_utils import run_bass_kernel_spmd as _run

    nc = _bacc.Bacc("TRN2", target_bir_lowering=False, num_devices=1)
    arrays, args = {}, []
    for name in _INS:
        a = _np.ascontiguousarray(inputs[name])
        arrays[f"in_{name}_dram"] = a
        args.append(nc.dram_tensor(f"in_{name}_dram", a.shape, _mybir.dt.from_np(a.dtype), kind="ExternalInput").ap())
    n = inputs["x"].shape[0]
    args.append(nc.dram_tensor("out_0_dram", (n + 128, 128), _mybir.dt.float32, kind="ExternalOutput").ap())
    gnn_program(nc, *args)
    r = _run(nc, [arrays], core_ids=[0])
    return r.results[0]["out_0_dram"][:n]
```

```python
from contextlib import ExitStack

import concourse.bass as bass
from concourse import mybir

F32 = mybir.dt.float32
BF16 = mybir.dt.bfloat16
I32 = mybir.dt.int32
ALU = mybir.AluOpType
ACT = mybir.ActivationFunctionType
AX_X = mybir.AxisListType.X

P = 128
D = 128
HEADS = 4
HD = D // HEADS
COLS_PER_IT = 4
ROWS = 8
NODES_PER_IT = P * ROWS
SLOPE = 0.2
EPS = 1e-5
BIG = 3.0e38


def gnn_program(nc, x, src, dst, bond, w_embed, a_src, a_dst, w_lin, bias0, w1, b1, w2, b2, wa, ba, out):
    N = x.shape[0]
    E = src.shape[0]
    BOND = bond.shape[1]
    COLS = -(-E // P)
    COLS += -COLS % COLS_PER_IT
    ITS = COLS // COLS_PER_IT
    FULL = E // COLS
    TAIL = E - FULL * COLS
    LAST = FULL
    assert FULL == P - 1 and 0 < TAIL < COLS and ITS % 2 == 1
    assert ITS == -(-N // NODES_PER_IT)
    PAD = N + P - 1

    def node0(it):
        return N - NODES_PER_IT if isinstance(it, int) and it == ITS - 1 else NODES_PER_IT * it

    def past(k):
        return not isinstance(k, int) or k > 0

    x1 = nc.dram_tensor("x1_rows", (N, D), F32, kind="Internal").ap()
    spill = nc.dram_tensor("base_rows", (P, COLS * D), F32, kind="Internal").ap()

    ctx = ExitStack()
    with ctx:
        def sb(name, shape, dt=F32):
            return ctx.enter_context(nc.sbuf_tensor(name, shape, dt))

        def sem(name):
            return ctx.enter_context(nc.semaphore(name))

        ps = [ctx.enter_context(nc.psum_tensor(f"bank{i}", [P, 512], F32)) for i in range(8)]

        H = sb("H", [P, COLS * D])
        BD = sb("BD", [P, COLS * BOND])
        XE = sb("XE", [P, 2, COLS_PER_IT, 2, D])
        XN = sb("XN", [P, 2, ROWS, D])
        R = sb("R", [P, 16, D])
        TS = sb("TS", [P, 2, 512])
        O = sb("O", [P, 2, ROWS, D])
        BS = sb("BS", [P, 2, COLS_PER_IT, D])
        key0i = sb("key0i", [P, COLS], I32)
        key1i = sb("key1i", [P, COLS], I32)
        nexti = sb("nexti", [P, 1], I32)
        gidx = sb("gidx", [P, COLS, 2], I32)
        sidx = sb("sidx", [P, COLS], I32)
        key0 = sb("key0", [P, COLS])
        key1 = sb("key1", [P, COLS])
        nextf = sb("nextf", [P, 1])
        same = sb("same", [P, COLS])
        nsame = sb("nsame", [P, COLS])
        hmask = sb("hmask", [P, COLS])
        bw = sb("bw", [P, COLS])
        Z = sb("Z", [P, COLS, HEADS])
        ix = sb("ix", [P, 2, COLS_PER_IT, 2], I32)
        ix3 = sb("ix3", [P, 3, COLS_PER_IT, 2], I32)
        sx = sb("sx", [P, 2, COLS_PER_IT], I32)
        ident = sb("ident", [P, P])
        ltri = sb("ltri", [P, P])
        utri = sb("utri", [P, P])
        ones = R[:, 10, :]
        epsc = sb("epsc", [P, 1])
        spare = sb("spare", [P, 1])
        wes = sb("wes", [P, D + HEADS])
        wls = sb("wls", [P, D + HEADS])
        w1s = sb("w1s", [P, 3, D])
        w2s = sb("w2s", [P, D])
        abr = R[:, 8:10, :]
        wabr = sb("wabr", [P, BOND])
        babr = sb("babr", [P, 1])
        b1c = sb("b1c", [P, 1])
        brow = TS[0:1, 0, 0:2 * D].rearrange("p (n d) -> p n d", n=2)
        b3 = sb("b3", [3, 2, 512], BF16)
        b3r = TS[0:1, 1, 256:512].bitcast(BF16)
        bt = TS[0:1, 1, 0:2 * D].rearrange("p (n d) -> p n d", n=2)
        on3 = sb("on3", [3, P], BF16)
        st = sb("st", [P, 16, 6])
        sa = sb("sa", [P, 3, 16])
        sm = sb("sm", [P, 16])
        sc = sb("sc", [P, 16])
        var = sb("var", [P, 3, 16])
        std = sb("std", [P, 3, 16])
        rstd = sb("rstd", [P, 3, 16])
        nmr = sb("nmr", [P, 3, 16])

        G4 = COLS_PER_IT

        def col(j):
            return bass.ds(j * D, D)

        ld_idx, ld_w, ld_bd = sem("ld_idx"), sem("ld_w"), sem("ld_bd")
        pads_set, tri_init, consts, zeroed, wchain, idx_done = (sem(n) for n in (
            "pads_set", "tri_init", "consts", "zeroed", "wchain", "idx_done"))
        dummy_rows, b_parts, ld_b3 = sem("dummy_rows"), sem("b_parts"), sem("ld_b3")
        with nc.Block() as block:
            @block.sync
            def _(sp):
                sp.wait_ge(pads_set, 3)
                for t, a in ((key0i, dst), (key1i, src)):
                    sp.dma_start(t[0:FULL, :], a[0:FULL * COLS].rearrange("(p j) -> p j", j=COLS)).then_inc(ld_idx, 16)
                    sp.dma_start(t[LAST:P, 0:TAIL], a[FULL * COLS:E].rearrange("(p j) -> p j", p=1)).then_inc(ld_idx, 16)
                with nc.allow_non_contiguous_dma(reason="one key per partition"):
                    sp.dma_start(nexti[0:FULL - 1, :],
                                 dst[COLS:FULL * COLS].rearrange("(p j) -> p j", j=COLS)[:, 0:1]).then_inc(ld_idx, 16)
                    sp.dma_start(nexti[FULL - 1:FULL, :],
                                 dst[FULL * COLS:FULL * COLS + 1].rearrange("(p j) -> p j", p=1)).then_inc(ld_idx, 16)
                sp.wait_ge(pads_set, 4)
                sp.wait_ge(b_parts, 1)
                part = [b3r[:, 0:2 * D], b3r[:, 2 * D:4 * D], TS[0:1, 0, 256:384].bitcast(BF16)]
                for n in range(3):
                    for layer in range(2):
                        for c in range(3 + layer):
                            sp.dma_start(b3[n:n + 1, layer, c * D:(c + 1) * D], part[n][:, layer * D:(layer + 1) * D]).then_inc(ld_b3, 16)
                sp.wait_ge(ld_b3, 16 * 21)
                sp.wait_ge(zeroed, 1)
                sp.dma_start(out[N:N + P, :], O[:, 0, 0, :]).then_inc(dummy_rows, 16)
                sp.wait_ge(dummy_rows, 16)

            @block.scalar
            def _(act):
                act.dma_start(wes[:, 0:D], w_embed).then_inc(ld_w, 16)
                act.dma_start(wls[:, 0:D], w_lin).then_inc(ld_w, 16)
                act.dma_start(abr[:, 0, :], a_src.rearrange("(o h) d -> o (h d)", o=1).to_broadcast([P, D])).then_inc(ld_w, 16)
                act.dma_start(abr[:, 1, :], a_dst.rearrange("(o h) d -> o (h d)", o=1).to_broadcast([P, D])).then_inc(ld_w, 16)
                act.dma_start(w1s[:, 0, :], w1[0:D, :]).then_inc(ld_w, 16)
                act.dma_start(w1s[:, 1, :], w1[D:2 * D, :]).then_inc(ld_w, 16)
                act.dma_start(w1s[0:BOND, 2, :], w1[2 * D:2 * D + BOND, :]).then_inc(ld_w, 16)
                act.dma_start(w2s[:, :], w2).then_inc(ld_w, 16)
                act.dma_start(wabr[:, :], wa.rearrange("c o -> o c").to_broadcast([P, BOND])).then_inc(ld_w, 16)
                act.dma_start(babr[:, :], ba.rearrange("(o c) -> o c", o=1).to_broadcast([P, 1])).then_inc(ld_w, 16)
                with nc.allow_non_contiguous_dma(reason="a bias per partition"):
                    act.dma_start(b1c[:, :], b1.rearrange("(p o) -> p o", o=1)).then_inc(ld_w, 16)
                act.dma_start(brow[:, 0, :], bias0.rearrange("(o c) -> o c", o=1)).then_inc(ld_w, 16)
                act.dma_start(brow[:, 1, :], b2.rearrange("(o c) -> o c", o=1)).then_inc(ld_w, 16)

            @block.gpsimd
            def _(pool):
                nc.gpsimd.memset(ones, 1.0).then_inc(tri_init, 1)
                pool.wait_ge(tri_init, 1)
                for t, pattern, mult, op in ((ident, [[-1, P]], 1, ALU.is_equal), (ltri, [[-1, P]], 1, ALU.is_gt),
                                             (utri, [[1, P]], -1, ALU.is_gt)):
                    nc.gpsimd.affine_select(out=t[:, :], in_=ones, compare_op=op, fill=0.0, base=0,
                                            pattern=pattern, channel_multiplier=mult).then_inc(consts, 1)
                nc.gpsimd.iota(spare[:, :], [[0, 1]], base=N, channel_multiplier=1,
                               allow_small_or_imprecise_dtypes=True).then_inc(consts, 1)

            @block.vector
            def _(dve):
                links = [0]

                def link(ins):
                    links[0] += 1
                    ins.then_inc(wchain, 1)
                    dve.wait_ge(wchain, links[0])

                nc.vector.memset(key0i[:, :], PAD).then_inc(pads_set, 1)
                nc.vector.memset(key1i[:, :], PAD).then_inc(pads_set, 1)
                nc.vector.memset(nexti[:, :], PAD).then_inc(pads_set, 1)
                nc.vector.memset(O[:, 0, 0, :], 0.0).then_inc(zeroed, 1)
                nc.vector.memset(epsc[:, :], EPS)
                nc.vector.memset(on3[:, :], 1.0)
                nc.vector.memset(b3[:, :, :], 0.0).then_inc(pads_set, 1)
                nc.vector.memset(same[:, :], 0.0)
                link(nc.vector.memset(nsame[:, :], 0.0))
                dve.wait_ge(ld_w, 16 * 13)
                for k, res in ((0, wes[:, D:D + HEADS]), (1, wls[:, D:D + HEADS])):
                    link(nc.vector.tensor_tensor(R[:, k, :], wes[:, 0:D], abr[:, k, :], ALU.mult))
                    link(nc.vector.tensor_reduce(res, R[:, k, :].rearrange("p (h d) -> p h d", h=HEADS), AX_X, ALU.add))
                part = [b3r[:, n * 2 * D:(n + 1) * 2 * D].rearrange("p (n d) -> p n d", n=2) for n in range(2)]
                part.append(TS[0:1, 0, 256:384].bitcast(BF16).rearrange("p (n d) -> p n d", n=2))
                link(nc.vector.tensor_copy(part[0], brow[:, :, :]))
                link(nc.vector.tensor_tensor(bt[:, :, :], brow[:, :, :], part[0], ALU.subtract))
                link(nc.vector.tensor_copy(part[1], bt[:, :, :]))
                link(nc.vector.tensor_tensor(bt[:, :, :], bt[:, :, :], part[1], ALU.subtract))
                nc.vector.tensor_copy(part[2], bt[:, :, :]).then_inc(b_parts, 1)
                dve.wait_ge(ld_idx, 16 * 6)
                nc.vector.tensor_copy(key0[:, :], key0i[:, :])
                nc.vector.tensor_copy(key1[:, :], key1i[:, :])
                link(nc.vector.tensor_copy(nextf[:, :], nexti[:, :]))
                nc.vector.tensor_scalar(gidx[:, :, 0], key1[:, :], float(N - 1), None, ALU.min)
                nc.vector.tensor_scalar(gidx[:, :, 1], key0[:, :], float(N - 1), None, ALU.min)
                nc.vector.tensor_scalar(hmask[:, :], key0[:, :], key0[:, 0:1], None, ALU.is_equal)
                link(nc.vector.tensor_tensor(same[:, 1:COLS], key0[:, 1:COLS], key0[:, 0:COLS - 1], ALU.is_equal))
                link(nc.vector.tensor_copy(nsame[:, 0:COLS - 1], same[:, 1:COLS]))
                far = float(2 ** 20)
                nc.vector.tensor_copy(R[:, 0:1, 0:COLS - D], nsame[:, D:COLS].rearrange("p (o c) -> p o c", o=1))
                link(nc.vector.tensor_copy(R[:, 4, 0:D], nsame[:, 0:D]))
                link(nc.vector.tensor_scalar(R[:, 0, COLS - D - 1:COLS - D], key0[:, COLS - 1:COLS], nextf[:, 0:1], None, ALU.is_equal))
                nc.vector.scalar_tensor_tensor(sidx[:, D:COLS], R[:, 0, 0:COLS - D], far, key0[:, D:COLS], ALU.mult, ALU.add)
                nc.vector.scalar_tensor_tensor(sidx[:, 0:D], R[:, 4, 0:D], far, key0[:, 0:D], ALU.mult, ALU.add).then_inc(idx_done, 1)
                dve.wait_ge(idx_done, 1)
                dve.wait_ge(consts, 4)

        def stats(tile_ap, t):
            return nc.vector.bn_stats(st[:, t, :], tile_ap)

        def moments(link, par, n, done):
            link(nc.vector.tensor_tensor(sm[:, 0:n], st[:, 0:n, 1], st[:, 0:n, 4], ALU.subtract))
            nc.vector.tensor_tensor(sa[:, par, 0:n], st[:, 0:n, 1], st[:, 0:n, 4], ALU.add)
            nc.vector.tensor_tensor(sc[:, 0:n], st[:, 0:n, 2], st[:, 0:n, 5], ALU.add)
            link(nc.vector.tensor_tensor(sm[:, 0:n], sm[:, 0:n], sm[:, 0:n], ALU.mult))
            nc.vector.scalar_tensor_tensor(var[:, par, 0:n], sm[:, 0:n], D / 4.0, sc[:, 0:n], ALU.mult, ALU.add).then_inc(done, 1)

        def scales(link, par, n, done):
            link(nc.vector.reciprocal(rstd[:, par, 0:n], std[:, par, 0:n]))
            nc.vector.scalar_tensor_tensor(nmr[:, par, 0:n], sa[:, par, 0:n], -0.5, rstd[:, par, 0:n],
                                           ALU.mult, ALU.mult).then_inc(done, 1)

        def root(par, n, done):
            nc.scalar.activation(std[:, par, 0:n], var[:, par, 0:n], ACT.Sqrt, bias=epsc[:, 0:1], scale=1.0 / D).then_inc(done, 1)

        def normalise(dst_ap, src_ap, par, t):
            return nc.scalar.activation(dst_ap, src_ap, ACT.Relu, bias=nmr[:, par, t:t + 1], scale=rstd[:, par, t:t + 1])

        def loop(eng, body):
            body(0, 0, 0)
            body(1, 1, 0)
            with eng.Fori(1, ITS // 2) as i:
                body(2 * i, 0, i)
                body(2 * i + 1, 1, i)
            body(ITS - 1, 0, ITS // 2)

        XE3 = BD[:, 0:3072].rearrange("p (u c s d) -> p u c s d", u=3, c=G4, s=2)
        XN3 = BD[:, 3072:6144].rearrange("p (u r d) -> p u r d", u=3, r=ROWS)
        O3 = BD[:, 6144:9216].rearrange("p (u r d) -> p u r d", u=3, r=ROWS)
        BS3 = BD[:, 9216:10752].rearrange("p (u c d) -> p u c d", u=3, c=G4)
        ld_xe = [[sem(f"l0_gathered{u}{c}") for c in range(G4)] for u in range(3)]
        ld_xn = [sem(f"l0_nodes{u}") for u in range(3)]
        st_o = [sem(f"l0_stored{u}") for u in range(3)]
        st_b = [sem(f"l0_spilled{u}") for u in range(3)]
        var_ready, std_ready, norm_ready, re_ready, rn_ready = (sem(n) for n in (
            "l0_var", "l0_std", "l0_norm", "l0_edge_rows", "l0_node_rows"))
        t_ready, ts_ready, mm_done, h_taken, out_taken, h_go = (sem(n) for n in (
            "l0_transposed", "l0_ts", "l0_products", "l0_h_taken", "l0_out_taken", "l0_h_go"))
        vchain, ix_ready, go = sem("l0_vchain"), sem("l0_ix"), sem("l0_go")
        psT, psA, psB = ps[0:2], ps[2:4], ps[4:6]
        CHUNKS = ((0, 5), (5, 11), (11, 16))

        def loop3(eng, body):
            for it in range(3):
                body(it, it, 0)
            with eng.Fori(1, ITS // 3 - 1) as i:
                for u in range(3):
                    body(3 * i + u, u, i)
            for it in range(3 * (ITS // 3 - 1), ITS):
                body(it, it % 3, it // 3)

        def upto(it, last):
            return not isinstance(it, int) or it <= last

        def step_past(it, g, n):
            return not isinstance(it, int) or G4 * it + g >= n

        with nc.Block() as block:
            @block.gpsimd
            def _(pool):
                lim = pool.to_reg(N - 1)

                def gather(it, u, k, released):
                    nc.gpsimd.tensor_copy(ix3[:, u, :, :], gidx[:, bass.ds(it * G4, G4), :]).then_inc(ix_ready, 1)
                    for c in range(G4):
                        if c == 0:
                            pool.wait_ge(ix_ready, it + 1)
                        if released:
                            pool.wait_ge(out_taken, G4 * (it - 3) + c + 1)
                        pool.sem_inc(go, 1)
                        for s in range(2):
                            pool.indirect_dma_start(XE3[:, u, c, s, :], None, x, bass.IndirectOffsetOnAxis(ix3[:, u, c, s:s + 1], 0),
                                                    bounds_check=lim, oob_is_err=False).then_inc(ld_xe[u][c], 16)

                def body(it, u, k):
                    if upto(it, ITS - 4):
                        pool.wait_ge(out_taken, G4 * it + 1)
                        gather(it + 3, u, k + 1, True)
                for n in range(3):
                    gather(n, n, 0, False)
                loop3(pool, body)

            @block.sync
            def _(sp):
                def load(it, u):
                    sp.dma_start(XN3[:, u, :, :], x[bass.ds(node0(it), NODES_PER_IT), :].rearrange("(p r) c -> p r c", r=ROWS)
                                 ).then_inc(ld_xn[u], 16)

                def body(it, u, k):
                    sp.wait_ge(out_taken, G4 * (it + 1))
                    if isinstance(it, int) and it == ITS - 1:
                        sp.wait_ge(st_o[(u + 2) % 3], 16 * (ITS // 3))
                    sp.dma_start(x1[bass.ds(node0(it), NODES_PER_IT), :].rearrange("(p r) c -> p r c", r=ROWS),
                                 O3[:, u, :, :]).then_inc(st_o[u], 16)
                    sp.dma_start(spill[:, bass.ds(it * G4 * D, G4 * D)],
                                 BS3[:, u, :, :].rearrange("p c d -> p (c d)")).then_inc(st_b[u], 16)
                    if upto(it, ITS - 4):
                        load(it + 3, u)
                for n in range(3):
                    load(n, n)
                loop3(sp, body)
                for u in range(3):
                    sp.wait_ge(st_o[u], 16 * (ITS // 3 + (u == 0)))
                    sp.wait_ge(st_b[u], 16 * (ITS // 3 + (u == 0)))

            @block.vector
            def _(dve):
                def linker(base):
                    n = [0]

                    def link(ins):
                        n[0] += 1
                        ins.then_inc(vchain, 1)
                        dve.wait_ge(vchain, base + n[0])
                    return link

                def measure(it, u, k, chunk, link):
                    for t in range(*CHUNKS[chunk]):
                        c, q = t // 4, t % 4
                        if t == 0:
                            dve.wait_ge(ld_xn[u], 16 * (k + 1))
                        if q == 0:
                            dve.wait_ge(ld_xe[u][c], 32 * (k + 1))
                        last = stats(XE3[:, u, c, q, :] if q < 2 else XN3[:, u, 2 * c + q - 2, :], t)
                    if chunk == 2:
                        link(last)
                        moments(link, u, 16, var_ready)

                def scale_edges(it, u, g):
                    if step_past(it, g, 4):
                        dve.wait_ge(t_ready, G4 * it + g - 3)
                    for s in range(2):
                        t = 4 * g + s
                        last = nc.vector.tensor_scalar(R[:, t, :], XE3[:, u, g, s, :], rstd[:, u, t:t + 1], nmr[:, u, t:t + 1],
                                                       ALU.mult, ALU.add)
                    last.then_inc(re_ready, 1)

                def take(it, u, k, g):
                    j = it * G4 + g
                    if g == 0 and past(k):
                        dve.wait_ge(st_o[u], 16 * k)
                        dve.wait_ge(st_b[u], 16 * k)
                    dve.wait_ge(mm_done, G4 * it + g + 1)
                    b = psB[g % 2]
                    nc.vector.tensor_tensor(BS3[:, u, g, :], b[:, 2 * D:3 * D], XE3[:, u, g, 1, :], ALU.add)
                    nc.vector.tensor_copy(Z[:, bass.ds(j, 1), :], b[:, 3 * D:3 * D + HEADS].rearrange("p (o h) -> p o h", o=1))
                    nc.vector.tensor_tensor(O3[:, u, 2 * g:2 * g + 2, :], b[:, 0:2 * D].rearrange("p (r c) -> p r c", r=2),
                                            XN3[:, u, 2 * g:2 * g + 2, :], ALU.add).then_inc(out_taken, 1)

                def body(it, u, k):
                    link = linker(4 * it + 4)
                    u1, k1 = (u + 1) % 3, k + (u == 2)
                    u2, k2 = (u + 2) % 3, k + (u >= 1)
                    for g in range(G4):
                        if step_past(it, g, 1):
                            if g == 0:
                                take(it - 1, (u + 2) % 3, k - (u == 0) if isinstance(it, int) else k, G4 - 1)
                            else:
                                take(it, u, k, g - 1)
                        if g < 2:
                            scale_edges(it, u, g + 2)
                        elif upto(it, ITS - 2):
                            if g == 2:
                                dve.wait_ge(std_ready, it + 2)
                                scales(link, u1, 16, norm_ready)
                                dve.wait_ge(norm_ready, it + 2)
                            scale_edges(it + 1, u1, g - 2)
                        if g < 2 and upto(it, ITS - 2):
                            measure(it + 1, u1, k1, g + 1, link)
                        if g == 3 and upto(it, ITS - 3):
                            measure(it + 2, u2, k2, 0, link)

                link = linker(0)
                for n in range(3):
                    measure(0, 0, 0, n, link)
                dve.wait_ge(std_ready, 1)
                scales(link, 0, 16, norm_ready)
                dve.wait_ge(norm_ready, 1)
                scale_edges(0, 0, 0)
                scale_edges(0, 0, 1)
                measure(1, 1, 0, 0, link)
                loop3(dve, body)
                take(ITS - 1, 0, ITS // 3, G4 - 1)

            @block.scalar
            def _(act):
                def take_h(it, g):
                    act.wait_ge(mm_done, G4 * it + g + 1)
                    act.sem_inc(h_go, 1)
                    nc.scalar.copy(H[:, col(it * G4 + g)], psA[g % 2][:, 0:D]).then_inc(h_taken, 1)

                def scale_nodes(it, u, g):
                    if step_past(it, g, 4):
                        act.wait_ge(t_ready, G4 * it + g - 3)
                    for r in range(2):
                        t = 4 * g + 2 + r
                        last = nc.scalar.activation(R[:, t, :], XN3[:, u, 2 * g + r, :], ACT.Identity, bias=nmr[:, u, t:t + 1],
                                                    scale=rstd[:, u, t:t + 1])
                    last.then_inc(rn_ready, 1)

                def body(it, u, k):
                    for g in range(G4):
                        act.wait_ge(t_ready, G4 * it + g + 1)
                        if step_past(it, g, 2):
                            act.wait_ge(mm_done, G4 * it + g - 1)
                        nc.scalar.activation(TS[:, g % 2, :], psT[g % 2][:, :], ACT.Relu).then_inc(ts_ready, 1)
                        if step_past(it, g, 1):
                            if g == 0:
                                take_h(it - 1, G4 - 1)
                            else:
                                take_h(it, g - 1)
                        if g < 2:
                            scale_nodes(it, u, g + 2)
                        elif upto(it, ITS - 2):
                            if g == 2:
                                act.wait_ge(var_ready, it + 2)
                                root((u + 1) % 3, 16, std_ready)
                                act.wait_ge(norm_ready, it + 2)
                            scale_nodes(it + 1, (u + 1) % 3, g - 2)

                act.wait_ge(var_ready, 1)
                root(0, 16, std_ready)
                act.wait_ge(norm_ready, 1)
                scale_nodes(0, 0, 0)
                scale_nodes(0, 0, 1)
                loop3(act, body)
                take_h(ITS - 1, G4 - 1)

            @block.tensor
            def _(pe):
                def flip(it, g):
                    pe.wait_ge(re_ready, G4 * it + g + 1)
                    pe.wait_ge(rn_ready, G4 * it + g + 1)
                    if step_past(it, g, 2):
                        pe.wait_ge(ts_ready, G4 * it + g - 1)
                    for q in range(4):
                        last = nc.tensor.transpose(psT[g % 2][:, q * D:(q + 1) * D], R[:, 4 * g + q, :], ident[:, :])
                    last.then_inc(t_ready, 1)

                def product(it, g):
                    a, b, t = psA[g % 2], psB[g % 2], TS[:, g % 2, :]
                    if step_past(it, g, 2):
                        pe.wait_ge(out_taken, G4 * it + g - 1)
                        pe.wait_ge(h_taken, G4 * it + g - 1)
                    nc.tensor.matmul(b[:, 0:3 * D + HEADS], on3[:, :], b3[:, 0, 0:3 * D + HEADS], start=True, stop=False, skip_group_check=True)
                    pe.wait_ge(ts_ready, G4 * it + g + 1)
                    nc.tensor.matmul(a[:, 0:D], t[:, 0:D], wes[:, 0:D], start=True, stop=True, skip_group_check=True)
                    nc.tensor.matmul(b[:, 3 * D:3 * D + HEADS], t[:, 0:D], wes[:, D:D + HEADS], start=False, stop=False, skip_group_check=True)
                    nc.tensor.matmul(b[:, 2 * D:3 * D + HEADS], t[:, D:2 * D], wls[:, :], start=False, stop=False, skip_group_check=True)
                    for r in range(2):
                        last = nc.tensor.matmul(b[:, r * D:(r + 1) * D], t[:, (2 + r) * D:(3 + r) * D], wls[:, 0:D],
                                                start=False, stop=(r == 1), skip_group_check=True)
                    last.then_inc(mm_done, 1)

                def body(it, u, k):
                    for g in range(G4):
                        if g < G4 - 1:
                            flip(it, g + 1)
                        elif upto(it, ITS - 2):
                            flip(it + 1, 0)
                        product(it, g)
                flip(0, 0)
                loop3(pe, body)

        def view(t, n, m):
            return t.rearrange("p (a b) -> p a b", b=m) if n else t
        Rf = R[:, :, :].rearrange("p t d -> p (t d)")
        Of = O[:, :, :, :].rearrange("p u r d -> p (u r d)")
        Xf = XE[:, :, :, :, :].rearrange("p u c s d -> p (u c s d)")
        Nf = XN[:, :, :, :].rearrange("p u r d -> p (u r d)")
        CH = COLS * HEADS
        F = Rf[:, 0:CH].rearrange("p (j h) -> p j h", h=HEADS)
        Q = Rf[:, CH:2 * CH].rearrange("p (j h) -> p j h", h=HEADS)
        M = Of[:, 0:CH].rearrange("p (j h) -> p j h", h=HEADS)
        pen = Of[:, CH:CH + COLS]
        penn = Of[:, CH + COLS:CH + 2 * COLS]
        tmask = Of[:, CH + 2 * COLS:CH + 3 * COLS]
        free_ = Of[:, CH + 3 * COLS:CH + 4 * COLS]
        rows = Xf[:, 0:10 * 256].rearrange("p (a q) -> p a q", q=256) if False else None
        keyr = Xf[:, 0:256]
        valr = Xf[:, 256:256 + HEADS * 256].rearrange("p (h q) -> p h q", q=256)
        m_h = Xf[:, 1280:1536]
        m_t = Xf[:, 1536:1792]
        work = Nf[:, 0:HEADS * 256].rearrange("p (h q) -> p h q", q=256)
        pm = Nf[:, 1024:1280]
        ends = Nf[:, 1280:1296]
        tot = Nf[:, 1296:1304].rearrange("p (s h) -> p s h", h=HEADS)
        carry_mask = Nf[:, 1408:1536]
        carry = Nf[:, 1536:1664]
        bwork = TS[:, :, :].rearrange("p u c -> p (u c)")
        zb = Of[:, CH + 4 * COLS:CH + 5 * COLS]
        BCH = 14
        s_v, s_ready, s_pe, s_exp, s_bw, s_sig, s_p4 = (sem(n) for n in (
            "sm_chain", "sm_ends", "sm_rows", "sm_exp", "sm_bond", "sm_sigmoid", "sm_run"))
        s_c = sem("sm_carry")
        bd_pads = sem("bd_pads")
        with nc.Block() as block:
            @block.sync
            def _(sp):
                sp.wait_ge(bd_pads, 1)
                sp.dma_start(BD[0:112, :], bond[0:112 * COLS, :].rearrange("(p j) c -> p (j c)", j=COLS)).then_inc(ld_bd, 16)
                sp.dma_start(BD[112:FULL, :], bond[112 * COLS:FULL * COLS, :].rearrange("(p j) c -> p (j c)", j=COLS)).then_inc(ld_bd, 16)
                sp.dma_start(BD[LAST:P, 0:TAIL * BOND], bond[FULL * COLS:E, :].rearrange("(p j) c -> p (j c)", p=1)).then_inc(ld_bd, 16)

            @block.gpsimd
            def _(pool):
                nc.gpsimd.memset(BD[96:P, :], 0.0).then_inc(bd_pads, 1)

            @block.tensor
            def _(pe):
                for r in range(3):
                    pe.wait_ge(s_ready, r + 1)
                    n = 2 if r == 0 else 2 * HEADS
                    for q in range(n):
                        c = (key0[:, 0:1], key0[:, COLS - 1:COLS])[q] if r == 0 else ends[:, q:q + 1]
                        last = nc.tensor.transpose(ps[3 * (r % 2) + q // 4][:, (q % 4) * P:(q % 4 + 1) * P],
                                                   c.to_broadcast([P, P]), ident[:, :])
                    last.then_inc(s_pe, 1)
                pe.wait_ge(s_ready, 4)
                nc.tensor.matmul(ps[6][:, 0:D], carry_mask, H[:, (COLS - 1) * D:COLS * D], start=True, stop=True).then_inc(s_c, 1)

            @block.scalar
            def _(act):
                act.wait_ge(s_exp, 1)
                nc.scalar.activation(Z[:, :, :], Z[:, :, :], ACT.Exp).then_inc(s_exp, 1)
                act.wait_ge(s_bw, 1)
                nc.scalar.activation(bw[:, :], zb, ACT.Sigmoid, bias=babr[:, 0:1]).then_inc(s_sig, 1)

            @block.vector
            def _(dve):
                links = [0]

                def link(ins):
                    links[0] += 1
                    ins.then_inc(s_v, 1)
                    dve.wait_ge(s_v, links[0])

                nc.vector.tensor_copy(pen[:, 0:1], key0[:, 0:1]).then_inc(s_ready, 1)
                for h in range(HEADS):
                    link(nc.vector.tensor_scalar(F[:, :, h], Z[:, :, h], SLOPE, None, ALU.mult))
                link(nc.vector.tensor_tensor(Z[:, :, :], Z[:, :, :], F[:, :, :], ALU.max))
                link(nc.vector.tensor_scalar(pen, same[:, :], -1.0, BIG, ALU.add, ALU.mult))
                nc.vector.tensor_scalar(penn, nsame[:, :], -1.0, BIG, ALU.add, ALU.mult)
                link(nc.vector.tensor_scalar(tmask, key0[:, :], key0[:, COLS - 1:COLS], None, ALU.is_equal))
                link(nc.vector.tensor_tensor(free_, hmask[:, :], tmask, ALU.max))
                link(nc.vector.tensor_scalar(free_, free_, -1.0, 1.0, ALU.mult, ALU.add))
                link(nc.vector.scalar_tensor_tensor(tmask, hmask[:, :], -1.0, tmask, ALU.mult, ALU.add))
                link(nc.vector.tensor_scalar(tmask, tmask, 0.0, None, ALU.max))

                for h in range(HEADS):
                    link(nc.vector.tensor_tensor_scan(F[:, :, h], pen, Z[:, :, h], -BIG, ALU.add, ALU.max))
                for h in range(HEADS):
                    link(nc.vector.tensor_tensor_scan(Q[:, ::-1, h], penn[:, ::-1], F[:, ::-1, h], 0.0, ALU.add, ALU.max))
                link(nc.vector.tensor_copy(ends[:, 0:HEADS], Q[:, 0, :]))
                dve.wait_ge(s_pe, 1)
                link(nc.vector.tensor_copy(keyr, ps[0][:, 0:256]))
                link(nc.vector.tensor_scalar(m_h, keyr, key0[:, 0:1], None, ALU.is_equal))
                link(nc.vector.tensor_scalar(m_t, keyr, key0[:, COLS - 1:COLS], None, ALU.is_equal))
                nc.vector.tensor_copy(ends[:, HEADS:2 * HEADS], Q[:, COLS - 1, :]).then_inc(s_ready, 1)

                def combine(bank0, r, is_max):
                    dve.wait_ge(s_pe, r)
                    for half in range(2):
                        link(nc.vector.tensor_copy(valr[:, :, half * P:(half + 1) * P],
                                                   ps[bank0 + half][:, :].rearrange("p (h q) -> p h q", q=P)))
                    for s, m in ((0, m_h), (1, m_t)):
                        for h in range(HEADS):
                            link(nc.vector.tensor_tensor(work[:, h, :], valr[:, h, :], m, ALU.mult))
                        if is_max:
                            link(nc.vector.tensor_scalar(pm, m, -1.0, BIG, ALU.add, ALU.mult))
                            for h in range(HEADS):
                                link(nc.vector.tensor_tensor(work[:, h, :], work[:, h, :], pm, ALU.add))
                        link(nc.vector.tensor_reduce(tot[:, s, :], work[:, :, :], AX_X, ALU.max if is_max else ALU.add))
                    for h in range(HEADS):
                        link(nc.vector.tensor_tensor(M[:, :, h], Q[:, :, h], free_, ALU.mult))
                        link(nc.vector.scalar_tensor_tensor(M[:, :, h], hmask[:, :], tot[:, 0, h:h + 1], M[:, :, h], ALU.mult, ALU.add))
                        link(nc.vector.scalar_tensor_tensor(M[:, :, h], tmask, tot[:, 1, h:h + 1], M[:, :, h], ALU.mult, ALU.add))

                combine(3, 2, True)
                nc.vector.tensor_tensor(Z[:, :, :], Z[:, :, :], M[:, :, :], ALU.subtract).then_inc(s_exp, 1)
                dve.wait_ge(s_exp, 2)
                for h in range(HEADS):
                    link(nc.vector.tensor_tensor_scan(F[:, :, h], same[:, :], Z[:, :, h], 0.0, ALU.mult, ALU.add))
                link(nc.vector.tensor_scalar(pen, nsame[:, :], -1.0, 1.0, ALU.mult, ALU.add))
                for h in range(HEADS):
                    link(nc.vector.tensor_tensor(F[:, :, h], F[:, :, h], pen, ALU.mult))
                for h in range(HEADS):
                    link(nc.vector.tensor_tensor_scan(Q[:, ::-1, h], nsame[:, ::-1], F[:, ::-1, h], 0.0, ALU.mult, ALU.add))
                link(nc.vector.tensor_copy(ends[:, 0:HEADS], Q[:, 0, :]))
                link(nc.vector.tensor_scalar(pm[:, 0:1], hmask[:, COLS - 1:COLS], -1.0, 1.0, ALU.mult, ALU.add))
                nc.vector.tensor_scalar(ends[:, HEADS:2 * HEADS], Q[:, COLS - 1, :], pm[:, 0:1], None, ALU.mult).then_inc(s_ready, 1)
                combine(0, 3, False)
                link(nc.vector.reciprocal(M[:, :, :], M[:, :, :]))
                link(nc.vector.tensor_tensor(Z[:, :, :], Z[:, :, :], M[:, :, :], ALU.mult))

                dve.wait_ge(ld_bd, 16 * 3)
                for b in range(COLS // BCH):
                    w = bwork[:, 0:BCH * BOND].rearrange("p (j c) -> p j c", c=BOND)
                    link(nc.vector.tensor_tensor(w, BD[:, b * BCH * BOND:(b + 1) * BCH * BOND].rearrange("p (j c) -> p j c", c=BOND),
                                                 wabr[:, :].unsqueeze(1).to_broadcast([P, BCH, BOND]), ALU.mult))
                    link(nc.vector.tensor_reduce(zb[:, b * BCH:(b + 1) * BCH], w, AX_X, ALU.add))
                nc.vector.tensor_copy(pm[:, 0:1], zb[:, 0:1]).then_inc(s_bw, 1)

                def run(it, base, first):
                    n = [0]

                    def step(ins):
                        n[0] += 1
                        ins.then_inc(s_p4, 1)
                        dve.wait_ge(s_p4, base + n[0])
                    hv = H[:, bass.ds(it * G4 * D, G4 * D)].rearrange("p (g d) -> p g d", d=HD)
                    pv = Z[:, bass.ds(it * G4, G4), :].rearrange("p j h -> p (j h)").unsqueeze(2).to_broadcast([P, G4 * HEADS, HD])
                    step(nc.vector.tensor_tensor(hv, hv, pv, ALU.mult))
                    for c in range(G4):
                        if first and c == 0:
                            continue
                        j = it * G4 + c
                        step(nc.vector.scalar_tensor_tensor(H[:, col(j)], H[:, col(j - 1)], same[:, bass.ds(j, 1)], H[:, col(j)],
                                                            ALU.mult, ALU.add))
                run(0, 0, True)
                with dve.Fori(1, ITS) as i:
                    run(i, 5 * i - 1, False)
                link(nc.vector.scalar_tensor_tensor(carry_mask, keyr[:, 0:P], key0[:, COLS - 1:COLS], utri[:, :], ALU.is_equal, ALU.mult))
                nc.vector.tensor_copy(pm[:, 0:1], keyr[:, 0:1]).then_inc(s_ready, 1)
                dve.wait_ge(s_c, 1)
                link(nc.vector.tensor_copy(carry, ps[6][:, 0:D]))
                dve.wait_ge(s_sig, 1)

        ld_b = [sem("sc_base0"), sem("sc_base1")]
        sc_done = [sem("sc_done0"), sem("sc_done1")]
        sc_rows, sc_chain, sc_ix, sc_go = (sem(n) for n in ("sc_rows", "sc_chain", "sc_ix", "sc_go"))
        W4 = XE[:, :, :, 0, :]
        with nc.Block() as block:
            @block.sync
            def _(sp):
                def body(it, u, k):
                    if past(k):
                        sp.wait_ge(sc_rows, it - 1)
                    sp.dma_start(BS[:, u, :, :].rearrange("p c d -> p (c d)"), spill[:, bass.ds(it * G4 * D, G4 * D)]).then_inc(ld_b[u], 16)
                loop(sp, body)

            @block.vector
            def _(dve):
                def body(it, u, k):
                    if past(k):
                        dve.wait_ge(sc_done[u], 16 * G4 * k)
                    for c in range(G4):
                        j = it * G4 + c
                        last = nc.vector.scalar_tensor_tensor(O[:, u, c, :], carry, hmask[:, bass.ds(j, 1)], H[:, col(j)],
                                                              ALU.mult, ALU.add)
                    last.then_inc(sc_chain, 1)
                    dve.wait_ge(sc_chain, it + 1)
                    dve.wait_ge(ld_b[u], 16 * (k + 1))
                    nc.vector.tensor_tensor(O[:, u, 0:G4, :], O[:, u, 0:G4, :], BS[:, u, :, :], ALU.add).then_inc(sc_rows, 1)
                loop(dve, body)

            @block.gpsimd
            def _(pool):
                lim = pool.to_reg(N - 1)

                def body(it, u, k):
                    if past(k):
                        pool.wait_ge(sc_done[u], 16 * G4 * k)
                    nc.gpsimd.tensor_copy(sx[:, u, :], sidx[:, bass.ds(it * G4, G4)]).then_inc(sc_ix, 1)
                    pool.wait_ge(sc_ix, it + 1)
                    pool.wait_ge(sc_rows, it + 1)
                    pool.sem_inc(sc_go, 1)
                    for c in range(G4):
                        pool.indirect_dma_start(x1, bass.IndirectOffsetOnAxis(sx[:, u, c:c + 1], 0), O[:, u, c, :], None,
                                                bounds_check=lim, oob_is_err=False).then_inc(sc_done[u], 16)
                loop(pool, body)
                for u in range(2):
                    pool.wait_ge(sc_done[u], 16 * G4 * (ITS // 2 + 1 - u))

        dn_ld = [sem("dn_nodes0"), sem("dn_nodes1")]
        dn_st = [sem("dn_stored0"), sem("dn_stored1")]
        dn_var, dn_std, dn_norm, dn_r, dn_o, dn_chain = (sem(n) for n in ("dn_var", "dn_std", "dn_norm", "dn_rows", "dn_out", "dn_chain"))
        with nc.Block() as block:
            @block.sync
            def _(sp):
                def load(it, u, k):
                    if past(k):
                        sp.wait_ge(dn_o, it - 1)
                    sp.dma_start(XN[:, u, :, :], x1[bass.ds(node0(it), NODES_PER_IT), :].rearrange("(p r) c -> p r c", r=ROWS)
                                 ).then_inc(dn_ld[u], 16)

                def store(it, u, k):
                    sp.wait_ge(dn_o, it + 1)
                    if isinstance(it, int) and it == ITS - 1:
                        sp.wait_ge(dn_st[1], 16 * (ITS // 2))
                    sp.dma_start(out[bass.ds(node0(it), NODES_PER_IT), :].rearrange("(p r) c -> p r c", r=ROWS),
                                 O[:, u, :, :]).then_inc(dn_st[u], 16)
                load(0, 0, 0)
                load(1, 1, 0)
                store(0, 0, 0)
                with sp.Fori(1, ITS // 2) as i:
                    load(2 * i, 0, i)
                    store(2 * i - 1, 1, i)
                    load(2 * i + 1, 1, i)
                    store(2 * i, 0, i)
                load(ITS - 1, 0, ITS // 2)
                store(ITS - 2, 1, ITS // 2)
                store(ITS - 1, 0, ITS // 2)
                for u in range(2):
                    sp.wait_ge(dn_st[u], 16 * (ITS // 2 + 1 - u))

            @block.vector
            def _(dve):
                def linker(base):
                    n = [0]

                    def link(ins):
                        n[0] += 1
                        ins.then_inc(dn_chain, 1)
                        dve.wait_ge(dn_chain, base + n[0])
                    return link

                def measure(it, u, k, link):
                    dve.wait_ge(dn_ld[u], 16 * (k + 1))
                    for r in range(ROWS):
                        last = stats(XN[:, u, r, :], r)
                    link(last)
                    moments(link, u, ROWS, dn_var)

                def body(it, u, k):
                    link = linker(4 * it + 3)
                    dve.wait_ge(dn_std, it + 1)
                    scales(link, u, ROWS, dn_norm)
                    if not (isinstance(it, int) and it == ITS - 1):
                        measure(it + 1, 1 - u, k + u, link)
                    if past(k):
                        dve.wait_ge(dn_st[u], 16 * k)
                    dve.wait_ge(dn_r, it + 1)
                    nc.vector.tensor_tensor(O[:, u, :, :], XN[:, u, :, :], R[:, bass.ds(ROWS * u, ROWS), :], ALU.add).then_inc(dn_o, 1)
                measure(0, 0, 0, linker(0))
                loop(dve, body)

            @block.scalar
            def _(act):
                def body(it, u, k):
                    act.wait_ge(dn_norm, it + 1)
                    if past(k):
                        act.wait_ge(dn_o, it - 1)
                    for r in range(ROWS):
                        last = normalise(R[:, ROWS * u + r, :], XN[:, u, r, :], u, r)
                    last.then_inc(dn_r, 1)
                    if not (isinstance(it, int) and it == ITS - 1):
                        act.wait_ge(dn_var, it + 2)
                        root(1 - u, ROWS, dn_std)
                act.wait_ge(dn_var, 1)
                root(0, ROWS, dn_std)
                loop(act, body)

        def h_part(n):
            return H[:, n * 512:(n + 1) * 512]
        HS, HDt, BT, HID, S, MS = (h_part(n) for n in range(6))
        UPD = [h_part(6), h_part(7)]
        RR = H[:, 4096:5120].rearrange("p (t d) -> p t d", d=D)
        junk = H[:, 5632:6144]
        cnt = H[:, 5248:5252]
        tt = H[:, 5252:5256]
        kcol = H[:, 5256:5260]
        bnd = H[:, 5264:5264 + G4 * BOND]
        ld_g = [sem("ms_gathered0"), sem("ms_gathered1")]
        (ms_var, ms_std, ms_norm, ms_src, ms_dst, ms_kb, ms_ts, ms_td, ms_hs, ms_hd, ms_bt, ms_s, ms_hid, ms_hidr, ms_msg,
         ms_scaled, ms_sum, ms_upd, ms_ix, ms_go, ms_sgo, ms_sx, ms_add, ms_chain, ms_col) = (sem("ms_" + n) for n in (
            "var", "std", "norm", "src", "dst", "kb", "ts", "td", "hs", "hd", "bt", "s", "hid", "hidr", "msg",
            "scaled", "sum", "upd", "ix", "go", "sgo", "sx", "add", "chain", "col"))
        bK, bB, bS, bD, bH, bM, bU = ps[0:7]
        with nc.Block() as block:
            @block.gpsimd
            def _(pool):
                lim = pool.to_reg(N - 1)
                limo = pool.to_reg(N + P - 1)

                def fetch_ix(it, u, k):
                    if past(k):
                        pool.wait_ge(ms_dst, it - 1)
                    nc.gpsimd.tensor_copy(ix[:, u, :, :], gidx[:, bass.ds(it * G4, G4), :]).then_inc(ms_ix, 1)
                    pool.wait_ge(ms_ix, it + 1)
                    pool.sem_inc(ms_go, 1)

                def fetch(u, c):
                    for s in range(2):
                        pool.indirect_dma_start(XE[:, u, c, s, :], None, x1, bass.IndirectOffsetOnAxis(ix[:, u, c, s:s + 1], 0),
                                                bounds_check=lim, oob_is_err=False).then_inc(ld_g[u], 16)

                def body(it, u, k):
                    more = not (isinstance(it, int) and it >= ITS - 2)
                    if more:
                        fetch_ix(it + 2, u, k + 1)
                    for c in range(G4):
                        if more:
                            fetch(u, c)
                        if c == 0:
                            pool.wait_ge(ms_sx, it + 1)
                            pool.wait_ge(ms_upd, it + 1)
                        if not (not past(k) and u == 0 and c == 0):
                            pool.wait_ge(ms_add, 16 * (G4 * it + c))
                        pool.sem_inc(ms_sgo, 1)
                        pool.indirect_dma_start(out, bass.IndirectOffsetOnAxis(sx[:, u, c:c + 1], 0), UPD[u][:, c * D:(c + 1) * D], None,
                                                bounds_check=limo, oob_is_err=True, compute_op=ALU.add).then_inc(ms_add, 16)
                for n in range(2):
                    fetch_ix(n, n, 0)
                    for c in range(G4):
                        fetch(n, c)
                body(0, 0, 0)
                body(1, 1, 0)
                with pool.Fori(1, ITS // 2 - 1) as i:
                    body(2 * i, 0, i)
                    body(2 * i + 1, 1, i)
                for it in range(ITS - 3, ITS):
                    body(it, it % 2, it // 2)
                pool.wait_ge(ms_add, 16 * COLS)

            @block.vector
            def _(dve):
                LINKS = 7

                def linker(base):
                    n = [0]

                    def link(ins):
                        n[0] += 1
                        ins.then_inc(ms_chain, 1)
                        dve.wait_ge(ms_chain, base + n[0])
                    return link

                def measure(it, u, k, link):
                    dve.wait_ge(ld_g[u], 16 * 2 * G4 * (k + 1))
                    for s in range(2):
                        for c in range(G4):
                            last = stats(XE[:, u, c, s, :], G4 * s + c)
                    link(last)
                    moments(link, u, 2 * G4, ms_var)

                def body(it, u, k):
                    first = not past(k) and u == 0
                    link = linker(LINKS * it + 3)
                    dve.wait_ge(ms_std, it + 1)
                    scales(link, u, 2 * G4, ms_norm)
                    dve.wait_ge(ms_kb, it + 1)
                    if not first:
                        dve.wait_ge(ms_sum, it)
                    for c in range(G4):
                        kc = key1[:, bass.ds(it * G4 + c, 1)]
                        nc.vector.tensor_scalar(S[:, c * D:(c + 1) * D], bK[:, c * D:(c + 1) * D], kc, None, ALU.is_equal)
                        last = nc.vector.scalar_tensor_tensor(junk[:, c * D:(c + 1) * D], bK[:, c * D:(c + 1) * D], kc, ltri[:, :], ALU.is_equal, ALU.mult,
                                                              accum_out=cnt[:, c:c + 1])
                    nc.vector.tensor_copy(BT[0:BOND, :], bB[0:BOND, :]).then_inc(ms_bt, 1)
                    dve.wait_ge(ms_bt, it + 1)
                    link(nc.vector.tensor_scalar(tt, cnt, 1.0, None, ALU.min))
                    k4 = key1[:, bass.ds(it * G4, G4)]
                    link(nc.vector.tensor_scalar(cnt, k4, -1.0, spare[:, 0:1], ALU.mult, ALU.add))
                    link(nc.vector.tensor_tensor(cnt, cnt, tt, ALU.mult))
                    if past(k):
                        dve.wait_ge(ms_add, 16 * G4 * (it - 1))
                    nc.vector.tensor_tensor(sx[:, u, :], cnt, k4, ALU.add).then_inc(ms_sx, 1)
                    if not (isinstance(it, int) and it == ITS - 1):
                        measure(it + 1, 1 - u, k + u, link)
                    dve.wait_ge(ms_msg, it + 1)
                    for c in range(G4):
                        last = nc.vector.tensor_scalar(MS[:, c * D:(c + 1) * D], bM[:, c * D:(c + 1) * D], bw[:, bass.ds(it * G4 + c, 1)],
                                                       None, ALU.mult)
                    last.then_inc(ms_scaled, 1)
                measure(0, 0, 0, linker(0))
                loop(dve, body)

            @block.scalar
            def _(act):
                def columns(it):
                    nc.scalar.copy(bnd, BD[:, bass.ds(it * G4 * BOND, G4 * BOND)])
                    nc.scalar.copy(kcol, key1[:, bass.ds(it * G4, G4)]).then_inc(ms_col, 1)

                def body(it, u, k):
                    first = not past(k) and u == 0
                    act.wait_ge(ms_norm, it + 1)
                    if not first:
                        act.wait_ge(ms_td, it)
                    for s, done in ((0, ms_src), (1, ms_dst)):
                        for c in range(G4):
                            last = normalise(RR[:, G4 * s + c, :], XE[:, u, c, s, :], u, G4 * s + c)
                        last.then_inc(done, 1)
                    if not first:
                        act.wait_ge(ms_hid, it)
                    act.wait_ge(ms_ts, it + 1)
                    nc.scalar.copy(HS, bS[:, :]).then_inc(ms_hs, 1)
                    act.wait_ge(ms_td, it + 1)
                    nc.scalar.copy(HDt, bD[:, :]).then_inc(ms_hd, 1)
                    act.wait_ge(ms_hid, it + 1)
                    if not first:
                        act.wait_ge(ms_msg, it)
                    nc.scalar.activation(HID, bH[:, :], ACT.Relu, bias=b1c[:, 0:1]).then_inc(ms_hidr, 1)
                    if not (isinstance(it, int) and it == ITS - 1):
                        act.wait_ge(ms_var, it + 2)
                        root(1 - u, 2 * G4, ms_std)
                    act.wait_ge(ms_sum, it + 1)
                    if past(k):
                        act.wait_ge(ms_add, 16 * G4 * (it - 1))
                    nc.scalar.copy(UPD[u], bU[:, :]).then_inc(ms_upd, 1)
                    if not (isinstance(it, int) and it == ITS - 1):
                        columns(it + 1)
                columns(0)
                act.wait_ge(ms_var, 1)
                root(0, 2 * G4, ms_std)
                loop(act, body)

            @block.tensor
            def _(pe):
                def body(it, u, k):
                    first = not past(k) and u == 0
                    if not first:
                        pe.wait_ge(ms_sx, it)
                        pe.wait_ge(ms_bt, it)
                    pe.wait_ge(ms_col, it + 1)
                    for c in range(G4):
                        nc.tensor.transpose(bK[:, c * D:(c + 1) * D], kcol[:, c:c + 1].to_broadcast([P, P]), ident[:, :])
                    for c in range(G4):
                        last = nc.tensor.transpose(bB[0:BOND, c * D:(c + 1) * D], bnd[:, c * BOND:(c + 1) * BOND], ident[:, :])
                    last.then_inc(ms_kb, 1)
                    pe.wait_ge(ms_src, it + 1)
                    if not first:
                        pe.wait_ge(ms_hs, it)
                    for c in range(G4):
                        last = nc.tensor.transpose(bS[:, c * D:(c + 1) * D], RR[:, c, :], ident[:, :])
                    last.then_inc(ms_ts, 1)
                    pe.wait_ge(ms_dst, it + 1)
                    if not first:
                        pe.wait_ge(ms_hd, it)
                    for c in range(G4):
                        last = nc.tensor.transpose(bD[:, c * D:(c + 1) * D], RR[:, G4 + c, :], ident[:, :])
                    last.then_inc(ms_td, 1)
                    pe.wait_ge(ms_bt, it + 1)
                    if not first:
                        pe.wait_ge(ms_hidr, it)
                    nc.tensor.matmul(bH[:, :], w1s[0:BOND, 2, :], BT[0:BOND, :], start=True, stop=False)
                    pe.wait_ge(ms_hs, it + 1)
                    nc.tensor.matmul(bH[:, :], w1s[:, 0, :], HS, start=False, stop=False)
                    pe.wait_ge(ms_hd, it + 1)
                    nc.tensor.matmul(bH[:, :], w1s[:, 1, :], HDt, start=False, stop=True).then_inc(ms_hid, 1)
                    pe.wait_ge(ms_hidr, it + 1)
                    if not first:
                        pe.wait_ge(ms_scaled, it)
                    nc.tensor.matmul(bM[:, :], on3[:, :], b3[:, 1, :], start=True, stop=False, skip_group_check=True)
                    for c in range(G4):
                        last = nc.tensor.matmul(bM[:, c * D:(c + 1) * D], HID[:, c * D:(c + 1) * D], w2s[:, :],
                                                start=False, stop=(c == G4 - 1), skip_group_check=True)
                    last.then_inc(ms_msg, 1)
                    pe.wait_ge(ms_scaled, it + 1)
                    if not first:
                        pe.wait_ge(ms_upd, it)
                    for c in range(G4):
                        last = nc.tensor.matmul(bU[:, c * D:(c + 1) * D], S[:, c * D:(c + 1) * D], MS[:, c * D:(c + 1) * D],
                                                start=True, stop=True, skip_group_check=True)
                    last.then_inc(ms_sum, 1)
                loop(pe, body)


_INS = ['x', 'src', 'dst', 'edge_attr_64', 'L0_gnn_W_embed', 'L0_gnn_a_src', 'L0_gnn_a_dst', 'L0_gnn_W_lin', 'L0_gnn_bias',
        'L1_gnn_W1', 'L1_gnn_b1', 'L1_gnn_W2', 'L1_gnn_b2', 'L1_gnn_Wa', 'L1_gnn_ba']


def kernel(**inputs):
    import numpy as _np
    import concourse.bacc as _bacc
    from concourse import mybir as _mybir
    from concourse.bass_utils import run_bass_kernel_spmd as _run

    nc = _bacc.Bacc("TRN2", target_bir_lowering=False, num_devices=1)
    arrays, args = {}, []
    for name in _INS:
        a = _np.ascontiguousarray(inputs[name])
        arrays[f"in_{name}_dram"] = a
        args.append(nc.dram_tensor(f"in_{name}_dram", a.shape, _mybir.dt.from_np(a.dtype), kind="ExternalInput").ap())
    n = inputs["x"].shape[0]
    args.append(nc.dram_tensor("out_0_dram", (n + 128, 128), _mybir.dt.float32, kind="ExternalOutput").ap())
    gnn_program(nc, *args)
    r = _run(nc, [arrays], core_ids=[0])
    return r.results[0]["out_0_dram"][:n]
```

```python
from contextlib import ExitStack

import concourse.bass as bass
from concourse import mybir

F32 = mybir.dt.float32
BF16 = mybir.dt.bfloat16
I32 = mybir.dt.int32
ALU = mybir.AluOpType
ACT = mybir.ActivationFunctionType
AX_X = mybir.AxisListType.X

P = 128
D = 128
HEADS = 4
HD = D // HEADS
COLS_PER_IT = 4
ROWS = 8
NODES_PER_IT = P * ROWS
SLOPE = 0.2
EPS = 1e-5
BIG = 3.0e38


def gnn_program(nc, x, src, dst, bond, w_embed, a_src, a_dst, w_lin, bias0, w1, b1, w2, b2, wa, ba, out):
    N = x.shape[0]
    E = src.shape[0]
    BOND = bond.shape[1]
    COLS = -(-E // P)
    COLS += -COLS % COLS_PER_IT
    ITS = COLS // COLS_PER_IT
    FULL = E // COLS
    TAIL = E - FULL * COLS
    LAST = FULL
    assert FULL == P - 1 and 0 < TAIL < COLS and ITS % 2 == 1
    assert ITS == -(-N // NODES_PER_IT)
    PAD = N + 3 * P - 1

    def node0(it):
        return N - NODES_PER_IT if isinstance(it, int) and it == ITS - 1 else NODES_PER_IT * it

    def past(k):
        return not isinstance(k, int) or k > 0

    x1 = nc.dram_tensor("x1_rows", (N, D), F32, kind="Internal").ap()
    ranked = nc.dram_tensor("ranked_edges", (P * COLS, 2), I32, kind="Internal").ap()
    spill = nc.dram_tensor("base_rows", (P, COLS * D), F32, kind="Internal").ap()

    ctx = ExitStack()
    with ctx:
        def sb(name, shape, dt=F32):
            return ctx.enter_context(nc.sbuf_tensor(name, shape, dt))

        def sem(name):
            return ctx.enter_context(nc.semaphore(name))

        ps = [ctx.enter_context(nc.psum_tensor(f"bank{i}", [P, 512], F32)) for i in range(8)]

        G4 = COLS_PER_IT
        H = sb("H", [P, COLS * D])
        BD = sb("BD", [P, COLS * BOND])
        XE = sb("XE", [P, 2, COLS_PER_IT, 2, D])
        XN = sb("XN", [P, 2, ROWS, D])
        R = sb("R", [P, 16, D])
        TS = sb("TS", [P, 2, 512])
        O = sb("O", [P, 2, ROWS, D])
        BS = sb("BS", [P, 2, COLS_PER_IT, D])
        key0i = BD[:, 0:COLS].bitcast(I32)
        key1i = BD[:, COLS:2 * COLS].bitcast(I32)
        nexti = sb("nexti", [P, 1], I32)
        gidx0 = BD[:, 12000:12000 + 2 * COLS].bitcast(I32).rearrange("p (j s) -> p j s", s=2)
        gidx = sb("gidx", [P, COLS, 2], I32)
        sidx = sb("sidx", [P, COLS], I32)
        hidx = sb("hidx", [P, 1], I32)
        hend = sb("hend", [P, COLS])
        Rw = R[:, :, :].rearrange("p t d -> p (t d)")
        key0 = sb("key0", [P, COLS])
        key1 = sb("key1", [P, COLS])
        nextf = sb("nextf", [P, 1])
        same = sb("same", [P, COLS])
        nsame = sb("nsame", [P, COLS])
        hmask = sb("hmask", [P, COLS])
        bw = sb("bw", [P, COLS])
        Z = sb("Z", [P, COLS, HEADS])
        ix3 = sb("ix3", [P, 3, COLS_PER_IT, 2], I32)
        ix = sb("ix", [P, 4, COLS_PER_IT], I32)
        ixs = sb("ixs", [P, 4, COLS_PER_IT], I32)
        sx = sb("sx", [P, 4, COLS_PER_IT], I32)
        ident = sb("ident", [P, P])
        ltri = sb("ltri", [P, 2 * P])
        utri = sb("utri", [P, P])
        ones = R[:, 10, :]
        epsc = sb("epsc", [P, 1])
        spare = sb("spare", [P, G4])
        wes = sb("wes", [P, D + HEADS])
        wls = sb("wls", [P, D + HEADS])
        w1s = sb("w1s", [P, 3, D])
        w2s = sb("w2s", [P, D])
        abr = R[:, 8:10, :]
        wabr = sb("wabr", [P, BOND])
        babr = sb("babr", [P, 1])
        b1c = sb("b1c", [P, 1])
        brow = TS[0:1, 0, 0:2 * D].rearrange("p (n d) -> p n d", n=2)
        b3 = sb("b3", [3, 2, 512], BF16)
        b3r = TS[0:1, 1, 256:512].bitcast(BF16)
        bt = TS[0:1, 1, 0:2 * D].rearrange("p (n d) -> p n d", n=2)
        on3 = sb("on3", [3, P], BF16)
        st = sb("st", [P, 16, 6])
        sa = sb("sa", [P, 3, 16])
        sm = sb("sm", [P, 16])
        sc = sb("sc", [P, 16])
        var = sb("var", [P, 3, 16])
        std = sb("std", [P, 3, 16])
        rstd = sb("rstd", [P, 3, 16])
        nmr = sb("nmr", [P, 3, 16])

        CH = 8
        NCH = P // CH
        count = BD[:, 512:512 + (2 * NCH + 1) * COLS].rearrange("p (n j) -> p n j", j=COLS)
        hit = BD[:, 8192:8192 + CH * COLS]
        lane = BD[:, 10240:10240 + COLS]
        left = BD[:, 10496:10496 + COLS]
        rank = BD[:, 10752:10752 + COLS].bitcast(I32)
        pairs = BD[:, 11008:11008 + 2 * COLS].bitcast(I32).rearrange("p (j s) -> p j s", s=2)
        rank1 = sb("rank1", [P, 1], I32)
        pair1 = sb("pair1", [P, 2], I32)
        unsorted = sb("unsorted", [P, 1], I32)
        down = sb("down", [P, 1])

        def col(j):
            return bass.ds(j * D, D)

        ld_idx, ld_w, ld_bd = sem("ld_idx"), sem("ld_w"), sem("ld_bd")
        pads_set, tri_init, consts, zeroed, wchain = (sem(n) for n in (
            "pads_set", "tri_init", "consts", "zeroed", "wchain"))
        (checked, summed, order_known, ld_all, ranks_ready, rank_copied, rank_go, ranked_out, ld_ranked, lanes_set, counted) = (
            sem(n) for n in ("checked", "summed", "order_known", "ld_all", "ranks_ready", "rank_copied", "rank_go", "ranked_out",
                             "ld_ranked", "lanes_set", "counted"))
        dummy_rows, b_parts, ld_b3 = sem("dummy_rows"), sem("b_parts"), sem("ld_b3")
        with nc.Block() as block:
            @block.sync
            def _(sp):
                sp.wait_ge(pads_set, 3)
                for t, a in ((key0i, dst), (key1i, src)):
                    sp.dma_start(t[0:FULL, :], a[0:FULL * COLS].rearrange("(p j) -> p j", j=COLS)).then_inc(ld_idx, 16)
                    sp.dma_start(t[LAST:P, 0:TAIL], a[FULL * COLS:E].rearrange("(p j) -> p j", p=1)).then_inc(ld_idx, 16)
                with nc.allow_non_contiguous_dma(reason="one key per partition"):
                    sp.dma_start(nexti[0:FULL - 1, :],
                                 dst[COLS:FULL * COLS].rearrange("(p j) -> p j", j=COLS)[:, 0:1]).then_inc(ld_idx, 16)
                    sp.dma_start(nexti[FULL - 1:FULL, :],
                                 dst[FULL * COLS:FULL * COLS + 1].rearrange("(p j) -> p j", p=1)).then_inc(ld_idx, 16)
                sp.wait_ge(order_known, 1)
                with sp.If(sp.value_load(unsorted[0:1, 0:1]) > 0):
                    sp.dma_start(H[:, 0:E].bitcast(I32), dst.rearrange("(o e) -> o e", o=1).to_broadcast([P, E])).then_inc(ld_all, 16)
                    sp.wait_ge(ranked_out, 16 * COLS)
                    sp.dma_start(pairs, ranked.rearrange("(p j) s -> p j s", j=COLS)).then_inc(ld_ranked, 16)
                    with nc.allow_non_contiguous_dma(reason="one key per partition"):
                        sp.dma_start(nexti[0:P - 1, :], ranked[COLS:P * COLS, :].rearrange("(p j) s -> p j s", j=COLS)[:, 0, 0:1]
                                     ).then_inc(ld_ranked, 16)
                sp.wait_ge(pads_set, 4)
                sp.wait_ge(zeroed, 1)
                for n in range(3):
                    sp.dma_start(out[N + n * P:N + (n + 1) * P, :], O[:, 0, 0, :]).then_inc(dummy_rows, 16)

            @block.scalar
            def _(act):
                act.dma_start(wes[:, 0:D], w_embed).then_inc(ld_w, 16)
                act.dma_start(wls[:, 0:D], w_lin).then_inc(ld_w, 16)
                act.dma_start(abr[:, 0, :], a_src.rearrange("(o h) d -> o (h d)", o=1).to_broadcast([P, D])).then_inc(ld_w, 16)
                act.dma_start(abr[:, 1, :], a_dst.rearrange("(o h) d -> o (h d)", o=1).to_broadcast([P, D])).then_inc(ld_w, 16)
                act.dma_start(w1s[:, 0, :], w1[0:D, :]).then_inc(ld_w, 16)
                act.dma_start(w1s[:, 1, :], w1[D:2 * D, :]).then_inc(ld_w, 16)
                act.dma_start(w1s[0:BOND, 2, :], w1[2 * D:2 * D + BOND, :]).then_inc(ld_w, 16)
                act.dma_start(w2s[:, :], w2).then_inc(ld_w, 16)
                act.dma_start(wabr[:, :], wa.rearrange("c o -> o c").to_broadcast([P, BOND])).then_inc(ld_w, 16)
                act.dma_start(babr[:, :], ba.rearrange("(o c) -> o c", o=1).to_broadcast([P, 1])).then_inc(ld_w, 16)
                with nc.allow_non_contiguous_dma(reason="a bias per partition"):
                    act.dma_start(b1c[:, :], b1.rearrange("(p o) -> p o", o=1)).then_inc(ld_w, 16)
                act.dma_start(brow[:, 0, :], bias0.rearrange("(o c) -> o c", o=1)).then_inc(ld_w, 16)
                act.dma_start(brow[:, 1, :], b2.rearrange("(o c) -> o c", o=1)).then_inc(ld_w, 16)

            @block.gpsimd
            def _(pool):
                nc.gpsimd.memset(ones, 1.0).then_inc(tri_init, 1)
                pool.wait_ge(tri_init, 1)
                for t, pattern, mult, op in ((ident, [[-1, P]], 1, ALU.is_equal), (ltri[:, P:2 * P], [[-1, P]], 1, ALU.is_gt),
                                             (utri, [[1, P]], -1, ALU.is_gt)):
                    nc.gpsimd.affine_select(out=t[:, 0:P], in_=ones, compare_op=op, fill=0.0, base=0,
                                            pattern=pattern, channel_multiplier=mult).then_inc(consts, 1)
                nc.gpsimd.memset(ltri[:, 0:P], 1.0).then_inc(consts, 1)
                nc.gpsimd.iota(spare[:, :], [[0, 2], [P, 2]], base=N, channel_multiplier=1,
                               allow_small_or_imprecise_dtypes=True).then_inc(consts, 1)
                nc.gpsimd.iota(lane, [[1, COLS]], base=0, channel_multiplier=0,
                               allow_small_or_imprecise_dtypes=True).then_inc(lanes_set, 1)
                pool.wait_ge(order_known, 1)
                with pool.If(pool.value_load(unsorted[0:1, 0:1]) > 0):
                    lim = pool.to_reg(P * COLS - 1)
                    pool.wait_ge(ranks_ready, 1)
                    with pool.Fori(0, COLS) as j:
                        nc.gpsimd.tensor_copy(rank1[:, :], rank[:, bass.ds(j, 1)]).then_inc(rank_copied, 1)
                        nc.gpsimd.tensor_copy(pair1[:, :], pairs[:, bass.ds(j, 1), :].rearrange("p o s -> p (o s)")).then_inc(rank_copied, 1)
                        pool.wait_ge(rank_copied, 2 * j + 2)
                        pool.sem_inc(rank_go, 1)
                        pool.indirect_dma_start(ranked, bass.IndirectOffsetOnAxis(rank1[:, 0:1], 0), pair1[:, :], None,
                                                bounds_check=lim, oob_is_err=True).then_inc(ranked_out, 16)
                        pool.wait_ge(ranked_out, 16 * j + 16)
                        pool.sem_inc(rank_go, 1)

            @block.tensor
            def _(pe):
                pe.wait_ge(consts, 4)
                pe.wait_ge(checked, 1)
                nc.tensor.matmul(ps[0][:, 0:1], ltri[:, 0:P], down[:, :], start=True, stop=True).then_inc(summed, 1)

            @block.vector
            def _(dve):
                links = [0]

                def link(ins):
                    links[0] += 1
                    ins.then_inc(wchain, 1)
                    dve.wait_ge(wchain, links[0])

                nc.vector.memset(key0i[:, :], PAD).then_inc(pads_set, 1)
                nc.vector.memset(key1i[:, :], PAD).then_inc(pads_set, 1)
                nc.vector.memset(nexti[:, :], PAD).then_inc(pads_set, 1)
                nc.vector.memset(O[:, 0, 0, :], 0.0).then_inc(zeroed, 1)
                nc.vector.memset(epsc[:, :], EPS)
                nc.vector.memset(on3[:, :], 1.0)
                nc.vector.memset(b3[:, :, :], 0.0).then_inc(pads_set, 1)
                nc.vector.memset(same[:, :], 0.0)
                link(nc.vector.memset(nsame[:, :], 0.0))
                dve.wait_ge(ld_idx, 16 * 6)
                nc.vector.tensor_copy(key0[:, :], key0i[:, :])
                nc.vector.tensor_copy(key1[:, :], key1i[:, :])
                link(nc.vector.tensor_copy(nextf[:, :], nexti[:, :]))
                nc.vector.tensor_tensor(Rw[:, 0:COLS - 1], key0[:, 1:COLS], key0[:, 0:COLS - 1], ALU.is_lt)
                link(nc.vector.tensor_tensor(Rw[:, COLS - 1:COLS], nextf[:, :], key0[:, COLS - 1:COLS], ALU.is_lt))
                nc.vector.tensor_reduce(down[:, :], Rw[:, 0:COLS], AX_X, ALU.max).then_inc(checked, 1)
                for g in (gidx0, gidx):
                    nc.vector.tensor_scalar(g[:, :, 0], key1[:, :], float(N - 1), None, ALU.min)
                    nc.vector.tensor_scalar(g[:, :, 1], key0[:, :], float(N - 1), None, ALU.min)
                dve.wait_ge(summed, 1)
                nc.vector.tensor_copy(unsorted[:, :], ps[0][:, 0:1]).then_inc(order_known, 1)
                dve.wait_ge(order_known, 1)
                with dve.If(dve.value_load(unsorted[0:1, 0:1]) > 0):
                    chained = [0]

                    def chain(ins):
                        chained[0] += 1
                        ins.then_inc(counted, 1)
                        dve.wait_ge(counted, chained[0])
                    dve.wait_ge(lanes_set, 1)
                    dve.wait_ge(ld_all, 16)
                    chain(nc.vector.tensor_copy(H[:, 0:E], H[:, 0:E].bitcast(I32)))
                    chain(nc.vector.memset(H[:, E:P * COLS], PAD))
                    chain(nc.vector.tensor_copy(pairs[:, :, 0], key0[:, :]))
                    chain(nc.vector.tensor_copy(pairs[:, :, 1], key1[:, :]))
                    base, per = chained[0], 2 * NCH + 2
                    with dve.Fori(0, COLS) as j:
                        k = key0[:, bass.ds(j, 1)]
                        n = [0]

                        def chain_j(ins):
                            n[0] += 1
                            ins.then_inc(counted, 1)
                            dve.wait_ge(counted, per * j + (base + n[0]))
                        hit3 = hit.rearrange("p (q j) -> p q j", j=COLS)
                        for c in range(NCH):
                            keys = H[:, c * CH * COLS:(c + 1) * CH * COLS]
                            before = ltri[:, P + c * CH:P + (c + 1) * CH].rearrange("p (q o) -> p q o", o=1).to_broadcast([P, CH, COLS])
                            chain_j(nc.vector.scalar_tensor_tensor(hit, keys, k, ltri[:, 0:1].to_broadcast([P, CH * COLS]),
                                                                   ALU.is_lt, ALU.mult, accum_out=count[:, c, bass.ds(j, 1)]))
                            chain_j(nc.vector.scalar_tensor_tensor(hit3, keys.rearrange("p (q j) -> p q j", j=COLS), k, before,
                                                                   ALU.is_equal, ALU.mult, accum_out=count[:, NCH + c, bass.ds(j, 1)]))
                        chain_j(nc.vector.tensor_scalar(left, lane, lane[:, bass.ds(j, 1)], None, ALU.is_lt))
                        chain_j(nc.vector.scalar_tensor_tensor(hit[:, 0:COLS], key0[:, :], k, left, ALU.is_equal, ALU.mult,
                                                               accum_out=count[:, 2 * NCH, bass.ds(j, 1)]))
                    for c in range(1, 2 * NCH + 1):
                        last = nc.vector.tensor_tensor(count[:, 0, :], count[:, 0, :], count[:, c, :], ALU.add)
                        last.then_inc(counted, 1)
                        dve.wait_ge(counted, base + per * COLS + c)
                    nc.vector.tensor_copy(rank, count[:, 0, :]).then_inc(ranks_ready, 1)
                    dve.wait_ge(ld_ranked, 32)
                    for t, res in ((nextf[:, :], nexti[:, :]), (key0[:, :], pairs[:, :, 0]), (left, pairs[:, :, 1])):
                        last = nc.vector.tensor_copy(t, res)
                    last.then_inc(counted, 1)
                    dve.wait_ge(counted, base + per * COLS + 2 * NCH + 1)
                    nc.vector.tensor_scalar(gidx0[:, :, 0], left, float(N - 1), None, ALU.min)
                    nc.vector.tensor_scalar(gidx0[:, :, 1], key0[:, :], float(N - 1), None, ALU.min)
                dve.wait_ge(consts, 5)

        def stats(tile_ap, t):
            return nc.vector.bn_stats(st[:, t, :], tile_ap)

        def moments(link, par, n, done):
            link(nc.vector.tensor_tensor(sm[:, 0:n], st[:, 0:n, 1], st[:, 0:n, 4], ALU.subtract))
            nc.vector.tensor_tensor(sa[:, par, 0:n], st[:, 0:n, 1], st[:, 0:n, 4], ALU.add)
            nc.vector.tensor_tensor(sc[:, 0:n], st[:, 0:n, 2], st[:, 0:n, 5], ALU.add)
            link(nc.vector.tensor_tensor(sm[:, 0:n], sm[:, 0:n], sm[:, 0:n], ALU.mult))
            nc.vector.scalar_tensor_tensor(var[:, par, 0:n], sm[:, 0:n], D / 4.0, sc[:, 0:n], ALU.mult, ALU.add).then_inc(done, 1)

        def scales(link, par, n, done):
            link(nc.vector.reciprocal(rstd[:, par, 0:n], std[:, par, 0:n]))
            nc.vector.scalar_tensor_tensor(nmr[:, par, 0:n], sa[:, par, 0:n], -0.5, rstd[:, par, 0:n],
                                           ALU.mult, ALU.mult).then_inc(done, 1)

        def root(par, n, done):
            nc.scalar.activation(std[:, par, 0:n], var[:, par, 0:n], ACT.Sqrt, bias=epsc[:, 0:1], scale=1.0 / D).then_inc(done, 1)

        def normalise(dst_ap, src_ap, par, t):
            return nc.scalar.activation(dst_ap, src_ap, ACT.Relu, bias=nmr[:, par, t:t + 1], scale=rstd[:, par, t:t + 1])

        def loop(eng, body):
            body(0, 0, 0)
            body(1, 1, 0)
            with eng.Fori(1, ITS // 2) as i:
                body(2 * i, 0, i)
                body(2 * i + 1, 1, i)
            body(ITS - 1, 0, ITS // 2)

        XE3 = BD[:, 0:3072].rearrange("p (u c s d) -> p u c s d", u=3, c=G4, s=2)
        XN3 = BD[:, 3072:6144].rearrange("p (u r d) -> p u r d", u=3, r=ROWS)
        O3 = BD[:, 6144:9216].rearrange("p (u r d) -> p u r d", u=3, r=ROWS)
        BS3 = BD[:, 9216:10752].rearrange("p (u c d) -> p u c d", u=3, c=G4)
        ld_xe = [[sem(f"l0_gathered{u}{c}") for c in range(G4)] for u in range(3)]
        ld_xn = [sem(f"l0_nodes{u}") for u in range(3)]
        st_o = [sem(f"l0_stored{u}") for u in range(3)]
        st_b = [sem(f"l0_spilled{u}") for u in range(3)]
        var_ready, std_ready, norm_ready, re_ready, rn_ready = (sem(n) for n in (
            "l0_var", "l0_std", "l0_norm", "l0_edge_rows", "l0_node_rows"))
        t_ready, ts_ready, mm_done, h_taken, out_taken, h_go = (sem(n) for n in (
            "l0_transposed", "l0_ts", "l0_products", "l0_h_taken", "l0_out_taken", "l0_h_go"))
        prepared, ix_go, vchain, ix_ready, go = sem("l0_prepared"), sem("l0_ix_go"), sem("l0_vchain"), sem("l0_ix"), sem("l0_go")
        psT, psA, psB = ps[0:2], ps[2:4], ps[4:6]
        CHUNKS = ((0, 8), (8, 13), (13, 16))

        def loop3(eng, body):
            for it in range(3):
                body(it, it, 0)
            with eng.Fori(1, ITS // 3 - 1) as i:
                for u in range(3):
                    body(3 * i + u, u, i)
            for it in range(3 * (ITS // 3 - 1), ITS):
                body(it, it % 3, it // 3)

        def upto(it, last):
            return not isinstance(it, int) or it <= last

        def step_past(it, g, n):
            return not isinstance(it, int) or G4 * it + g >= n

        with nc.Block() as block:
            @block.gpsimd
            def _(pool):
                lim = pool.to_reg(N - 1)

                def gather(it, u, k, released):
                    for c in range(G4):
                        if c == 0:
                            pool.wait_ge(ix_ready, it + 1)
                        if released:
                            pool.wait_ge(out_taken, G4 * (it - 3) + c + 1)
                        pool.sem_inc(go, 1)
                        for s in range(2):
                            pool.indirect_dma_start(XE3[:, u, c, s, :], None, x, bass.IndirectOffsetOnAxis(ix3[:, u, c, s:s + 1], 0),
                                                    bounds_check=lim, oob_is_err=False).then_inc(ld_xe[u][c], 16)

                def body(it, u, k):
                    if upto(it, ITS - 4):
                        pool.wait_ge(out_taken, G4 * it + 1)
                        gather(it + 3, u, k + 1, True)
                for n in range(3):
                    gather(n, n, 0, False)
                loop3(pool, body)

            @block.sync
            def _(sp):
                def load(it, u):
                    sp.dma_start(XN3[:, u, :, :], x[bass.ds(node0(it), NODES_PER_IT), :].rearrange("(p r) c -> p r c", r=ROWS)
                                 ).then_inc(ld_xn[u], 16)

                def body(it, u, k):
                    sp.wait_ge(out_taken, G4 * (it + 1))
                    if isinstance(it, int) and it == ITS - 1:
                        sp.wait_ge(st_o[(u + 2) % 3], 16 * (ITS // 3))
                    sp.dma_start(x1[bass.ds(node0(it), NODES_PER_IT), :].rearrange("(p r) c -> p r c", r=ROWS),
                                 O3[:, u, :, :]).then_inc(st_o[u], 16)
                    sp.dma_start(spill[:, bass.ds(it * G4 * D, G4 * D)],
                                 BS3[:, u, :, :].rearrange("p c d -> p (c d)")).then_inc(st_b[u], 16)
                    if upto(it, ITS - 4):
                        load(it + 3, u)
                for n in range(3):
                    load(n, n)
                sp.wait_ge(b_parts, 1)
                part = [b3r[:, 0:2 * D], b3r[:, 2 * D:4 * D], TS[0:1, 0, 256:384].bitcast(BF16)]
                for n in range(3):
                    for layer in range(2):
                        c = 3 + layer
                        sp.dma_start(b3[n:n + 1, layer, 0:c * D].rearrange("p (c d) -> p c d", d=D),
                                     part[n][:, layer * D:(layer + 1) * D].unsqueeze(1).to_broadcast([1, c, D])).then_inc(ld_b3, 16)
                loop3(sp, body)

            @block.vector
            def _(dve):
                links = [0]

                def link(ins):
                    links[0] += 1
                    ins.then_inc(prepared, 1)
                    dve.wait_ge(prepared, links[0])

                nc.vector.tensor_scalar(hmask[:, :], key0[:, :], key0[:, 0:1], None, ALU.is_equal)
                link(nc.vector.tensor_tensor(same[:, 1:COLS], key0[:, 1:COLS], key0[:, 0:COLS - 1], ALU.is_equal))
                link(nc.vector.tensor_copy(nsame[:, 0:COLS - 1], same[:, 1:COLS]))
                far = float(2 ** 20)
                e, he = Rw[:, 0:COLS], Rw[:, 256:256 + COLS]
                nc.vector.tensor_scalar(e[:, 0:COLS - 1], nsame[:, 0:COLS - 1], -1.0, 1.0, ALU.mult, ALU.add)
                link(nc.vector.tensor_scalar(e[:, COLS - 1:COLS], key0[:, COLS - 1:COLS], nextf[:, 0:1], None, ALU.not_equal))
                link(nc.vector.tensor_tensor(hend[:, :], e, hmask[:, :], ALU.mult))
                nc.vector.tensor_reduce(nextf[:, :], hend[:, :], AX_X, ALU.add)
                link(nc.vector.tensor_tensor(he, e, hend[:, :], ALU.subtract))
                link(nc.vector.tensor_scalar(he, he, -far, far, ALU.mult, ALU.add))
                link(nc.vector.tensor_scalar(nextf[:, :], nextf[:, :], -far, far, ALU.mult, ALU.add))
                nc.vector.tensor_tensor(hidx[:, :], nextf[:, :], key0[:, 0:1], ALU.add)
                link(nc.vector.tensor_tensor(sidx[:, :], he, key0[:, :], ALU.add))
                dve.wait_ge(ld_w, 16 * 13)
                for k, res in ((0, wes[:, D:D + HEADS]), (1, wls[:, D:D + HEADS])):
                    link(nc.vector.tensor_tensor(R[:, k, :], wes[:, 0:D], abr[:, k, :], ALU.mult))
                    link(nc.vector.tensor_reduce(res, R[:, k, :].rearrange("p (h d) -> p h d", h=HEADS), AX_X, ALU.add))
                part = [b3r[:, n * 2 * D:(n + 1) * 2 * D].rearrange("p (n d) -> p n d", n=2) for n in range(2)]
                part.append(TS[0:1, 0, 256:384].bitcast(BF16).rearrange("p (n d) -> p n d", n=2))
                link(nc.vector.tensor_copy(part[0], brow[:, :, :]))
                link(nc.vector.tensor_tensor(bt[:, :, :], brow[:, :, :], part[0], ALU.subtract))
                link(nc.vector.tensor_copy(part[1], bt[:, :, :]))
                link(nc.vector.tensor_tensor(bt[:, :, :], bt[:, :, :], part[1], ALU.subtract))
                nc.vector.tensor_copy(part[2], bt[:, :, :]).then_inc(b_parts, 1)
                dve.wait_ge(b_parts, 1)

                def linker(base):
                    n = [0]

                    def link(ins):
                        n[0] += 1
                        ins.then_inc(vchain, 1)
                        dve.wait_ge(vchain, base + n[0])
                    return link

                def measure(it, u, k, chunk, link):
                    for t in range(*CHUNKS[chunk]):
                        c, q = t // 4, t % 4
                        if t == 0:
                            dve.wait_ge(ld_xn[u], 16 * (k + 1))
                        if q == 0:
                            dve.wait_ge(ld_xe[u][c], 32 * (k + 1))
                        last = stats(XE3[:, u, c, q, :] if q < 2 else XN3[:, u, 2 * c + q - 2, :], t)
                    if chunk == 2:
                        link(last)
                        moments(link, u, 16, var_ready)

                def scale_edges(it, u, g):
                    if step_past(it, g, 4):
                        dve.wait_ge(t_ready, G4 * it + g - 3)
                    for s in range(g % 2, 2):
                        t = 4 * g + s
                        last = nc.vector.tensor_scalar(R[:, t, :], XE3[:, u, g, s, :], rstd[:, u, t:t + 1], nmr[:, u, t:t + 1],
                                                       ALU.mult, ALU.add)
                    last.then_inc(re_ready, 1)

                def take(it, u, k, g):
                    j = it * G4 + g
                    if g == 0 and past(k):
                        dve.wait_ge(st_o[u], 16 * k)
                        dve.wait_ge(st_b[u], 16 * k)
                    dve.wait_ge(mm_done, G4 * it + g + 1)
                    b = psB[g % 2]
                    nc.vector.tensor_tensor(BS3[:, u, g, :], b[:, 2 * D:3 * D], XE3[:, u, g, 1, :], ALU.add)
                    nc.vector.tensor_copy(Z[:, bass.ds(j, 1), :], b[:, 3 * D:3 * D + HEADS].rearrange("p (o h) -> p o h", o=1))
                    nc.vector.tensor_tensor(O3[:, u, 2 * g:2 * g + 2, :], b[:, 0:2 * D].rearrange("p (r c) -> p r c", r=2),
                                            XN3[:, u, 2 * g:2 * g + 2, :], ALU.add).then_inc(out_taken, 1)

                def body(it, u, k):
                    link = linker(4 * it + 4)
                    u1, k1 = (u + 1) % 3, k + (u == 2)
                    u2, k2 = (u + 2) % 3, k + (u >= 1)
                    for g in range(G4):
                        if step_past(it, g, 1):
                            if g == 0:
                                take(it - 1, (u + 2) % 3, k - (u == 0) if isinstance(it, int) else k, G4 - 1)
                            else:
                                take(it, u, k, g - 1)
                        if g < 2:
                            scale_edges(it, u, g + 2)
                        elif upto(it, ITS - 2):
                            if g == 2:
                                dve.wait_ge(std_ready, it + 2)
                                scales(link, u1, 16, norm_ready)
                                dve.wait_ge(norm_ready, it + 2)
                            scale_edges(it + 1, u1, g - 2)
                        if g < 2 and upto(it, ITS - 2):
                            measure(it + 1, u1, k1, g + 1, link)
                        if g == 3 and upto(it, ITS - 3):
                            measure(it + 2, u2, k2, 0, link)

                link = linker(0)
                for n in range(3):
                    measure(0, 0, 0, n, link)
                dve.wait_ge(std_ready, 1)
                scales(link, 0, 16, norm_ready)
                dve.wait_ge(norm_ready, 1)
                scale_edges(0, 0, 0)
                scale_edges(0, 0, 1)
                measure(1, 1, 0, 0, link)
                loop3(dve, body)
                take(ITS - 1, 0, ITS // 3, G4 - 1)

            @block.scalar
            def _(act):
                def indices(it, u):
                    act.sem_inc(ix_go, 1)
                    nc.scalar.copy(ix3[:, u, :, :], gidx0[:, bass.ds(it * G4, G4), :]).then_inc(ix_ready, 1)

                def take_h(it, g):
                    act.wait_ge(mm_done, G4 * it + g + 1)
                    act.sem_inc(h_go, 1)
                    nc.scalar.copy(H[:, col(it * G4 + g)], psA[g % 2][:, 0:D]).then_inc(h_taken, 1)

                def scale_nodes(it, u, g):
                    if step_past(it, g, 4):
                        act.wait_ge(t_ready, G4 * it + g - 3)
                    if g % 2:
                        t = 4 * g
                        nc.scalar.activation(R[:, t, :], XE3[:, u, g, 0, :], ACT.Identity, bias=nmr[:, u, t:t + 1],
                                             scale=rstd[:, u, t:t + 1])
                    for r in range(2):
                        t = 4 * g + 2 + r
                        last = nc.scalar.activation(R[:, t, :], XN3[:, u, 2 * g + r, :], ACT.Identity, bias=nmr[:, u, t:t + 1],
                                                    scale=rstd[:, u, t:t + 1])
                    last.then_inc(rn_ready, 1)

                def body(it, u, k):
                    for g in range(G4):
                        act.wait_ge(t_ready, G4 * it + g + 1)
                        if step_past(it, g, 2):
                            act.wait_ge(mm_done, G4 * it + g - 1)
                        nc.scalar.activation(TS[:, g % 2, :], psT[g % 2][:, :], ACT.Relu).then_inc(ts_ready, 1)
                        if step_past(it, g, 1):
                            if g == 0:
                                take_h(it - 1, G4 - 1)
                            else:
                                take_h(it, g - 1)
                        if g < 2:
                            scale_nodes(it, u, g + 2)
                        elif upto(it, ITS - 2):
                            if g == 2 and upto(it, ITS - 4):
                                indices(it + 3, u)
                            if g == 2:
                                act.wait_ge(var_ready, it + 2)
                                root((u + 1) % 3, 16, std_ready)
                                act.wait_ge(norm_ready, it + 2)
                            scale_nodes(it + 1, (u + 1) % 3, g - 2)

                for n in range(3):
                    indices(n, n)
                act.wait_ge(var_ready, 1)
                root(0, 16, std_ready)
                act.wait_ge(norm_ready, 1)
                scale_nodes(0, 0, 0)
                scale_nodes(0, 0, 1)
                act.wait_ge(ld_b3, 16 * 6)
                loop3(act, body)
                take_h(ITS - 1, G4 - 1)

            @block.tensor
            def _(pe):
                def flip(it, g):
                    pe.wait_ge(re_ready, G4 * it + g + 1)
                    pe.wait_ge(rn_ready, G4 * it + g + 1)
                    if step_past(it, g, 2):
                        pe.wait_ge(ts_ready, G4 * it + g - 1)
                    for q in range(4):
                        last = nc.tensor.transpose(psT[g % 2][:, q * D:(q + 1) * D], R[:, 4 * g + q, :], ident[:, :])
                    last.then_inc(t_ready, 1)

                def product(it, g):
                    a, b, t = psA[g % 2], psB[g % 2], TS[:, g % 2, :]
                    if step_past(it, g, 2):
                        pe.wait_ge(out_taken, G4 * it + g - 1)
                        pe.wait_ge(h_taken, G4 * it + g - 1)
                    nc.tensor.matmul(b[:, 0:3 * D + HEADS], on3[:, :], b3[:, 0, 0:3 * D + HEADS], start=True, stop=False, skip_group_check=True)
                    pe.wait_ge(ts_ready, G4 * it + g + 1)
                    nc.tensor.matmul(a[:, 0:D], t[:, 0:D], wes[:, 0:D], start=True, stop=True, skip_group_check=True)
                    nc.tensor.matmul(b[:, 3 * D:3 * D + HEADS], t[:, 0:D], wes[:, D:D + HEADS], start=False, stop=False, skip_group_check=True)
                    nc.tensor.matmul(b[:, 2 * D:3 * D + HEADS], t[:, D:2 * D], wls[:, :], start=False, stop=False, skip_group_check=True)
                    for r in range(2):
                        last = nc.tensor.matmul(b[:, r * D:(r + 1) * D], t[:, (2 + r) * D:(3 + r) * D], wls[:, 0:D],
                                                start=False, stop=(r == 1), skip_group_check=True)
                    last.then_inc(mm_done, 1)

                def body(it, u, k):
                    for g in range(G4):
                        if g < G4 - 1:
                            flip(it, g + 1)
                        elif upto(it, ITS - 2):
                            flip(it + 1, 0)
                        product(it, g)
                flip(0, 0)
                pe.wait_ge(ld_b3, 16 * 6)
                loop3(pe, body)

        Rf = R[:, :, :].rearrange("p t d -> p (t d)")
        Of = O[:, :, :, :].rearrange("p u r d -> p (u r d)")
        Xf = XE[:, :, :, :, :].rearrange("p u c s d -> p (u c s d)")
        Nf = XN[:, :, :, :].rearrange("p u r d -> p (u r d)")
        CH = COLS * HEADS
        F = Rf[:, 0:CH].rearrange("p (j h) -> p j h", h=HEADS)
        Q = Rf[:, CH:2 * CH].rearrange("p (j h) -> p j h", h=HEADS)
        M = Of[:, 0:CH].rearrange("p (j h) -> p j h", h=HEADS)
        pen = Of[:, CH:CH + COLS]
        penn = Of[:, CH + COLS:CH + 2 * COLS]
        tmask = Of[:, CH + 2 * COLS:CH + 3 * COLS]
        free_ = Of[:, CH + 3 * COLS:CH + 4 * COLS]
        keyr = BS[:, :, :, :].rearrange("p u c d -> p (u c d)")[:, 0:256]
        m_h = TS[:, 0, 0:256]
        m_t = TS[:, 0, 256:512]
        p_h = TS[:, 1, 0:256]
        p_t = TS[:, 1, 256:512]
        work = Xf.rearrange("p (s h q) -> p s h q", s=2, q=256)
        pm = Nf[:, 1024:1280]
        ends = Nf[:, 1280:1296]
        tot = Nf[:, 1296:1304].rearrange("p (s h) -> p s h", h=HEADS)
        carry_mask = Nf[:, 1408:1536]
        headrow = Nf[:, 1536:1664]
        tick = Nf[:, 1664:1665]
        bwork = TS[:, :, 0:G4 * BOND].rearrange("p u (c b) -> p u c b", b=BOND)
        zb = Nf[:, 1700:1700 + COLS]
        s_v, s_ready, s_pe, s_exp = (sem(n) for n in ("sm_chain", "sm_ends", "sm_rows", "sm_exp"))
        bd_pads = sem("bd_pads")
        with nc.Block() as block:
            @block.sync
            def _(sp):
                sp.wait_ge(dummy_rows, 48)
                for u in range(3):
                    sp.wait_ge(st_o[u], 16 * (ITS // 3 + (u == 0)))
                    sp.wait_ge(st_b[u], 16 * (ITS // 3 + (u == 0)))
                sp.dma_start(BD[0:48, :], bond[0:48 * COLS, :].rearrange("(p j) c -> p (j c)", j=COLS)).then_inc(ld_bd, 16)
                sp.dma_start(BD[48:96, :], bond[48 * COLS:96 * COLS, :].rearrange("(p j) c -> p (j c)", j=COLS)).then_inc(ld_bd, 16)
                sp.wait_ge(bd_pads, 1)
                sp.dma_start(BD[96:FULL, :], bond[96 * COLS:FULL * COLS, :].rearrange("(p j) c -> p (j c)", j=COLS)).then_inc(ld_bd, 16)
                sp.dma_start(BD[LAST:P, 0:TAIL * BOND], bond[FULL * COLS:E, :].rearrange("(p j) c -> p (j c)", p=1)).then_inc(ld_bd, 16)

            @block.gpsimd
            def _(pool):
                for u in range(3):
                    pool.wait_ge(st_o[u], 16 * (ITS // 3 + (u == 0)))
                    pool.wait_ge(st_b[u], 16 * (ITS // 3 + (u == 0)))
                nc.gpsimd.memset(BD[96:P, TAIL * BOND:COLS * BOND], 0.0).then_inc(bd_pads, 1)

            @block.tensor
            def _(pe):
                for r in range(3):
                    if r > 0:
                        pe.wait_ge(s_ready, r)
                    n = 2 if r == 0 else 2 * HEADS
                    for q in range(n):
                        c = (key0[:, 0:1], key0[:, COLS - 1:COLS])[q] if r == 0 else ends[:, q:q + 1]
                        last = nc.tensor.transpose(ps[3 * (r % 2) + q // 4][:, (q % 4) * P:(q % 4 + 1) * P],
                                                   c.to_broadcast([P, P]), ident[:, :])
                    last.then_inc(s_pe, 1)

            @block.scalar
            def _(act):
                act.wait_ge(s_exp, 1)
                nc.scalar.activation(Z[:, :, :], Z[:, :, :], ACT.Exp).then_inc(s_exp, 1)

            @block.vector
            def _(dve):
                links = [0]

                def link(ins):
                    links[0] += 1
                    ins.then_inc(s_v, 1)
                    dve.wait_ge(s_v, links[0])

                nc.vector.scalar_tensor_tensor(Z[:, :, :], Z[:, :, :], SLOPE, Z[:, :, :], ALU.mult, ALU.max)
                nc.vector.tensor_scalar(penn, nsame[:, :], -1.0, BIG, ALU.add, ALU.mult)
                nc.vector.tensor_scalar(tmask, key0[:, :], key0[:, COLS - 1:COLS], None, ALU.is_equal)
                link(nc.vector.tensor_scalar(pen, same[:, :], -1.0, BIG, ALU.add, ALU.mult))
                link(nc.vector.tensor_tensor(free_, hmask[:, :], tmask, ALU.max))
                link(nc.vector.scalar_tensor_tensor(tmask, hmask[:, :], -1.0, tmask, ALU.mult, ALU.add))
                nc.vector.tensor_scalar(free_, free_, -1.0, 1.0, ALU.mult, ALU.add)
                nc.vector.tensor_scalar(tmask, tmask, 0.0, None, ALU.max)

                for h in range(HEADS):
                    last = nc.vector.tensor_tensor_scan(F[:, :, h], pen, Z[:, :, h], -BIG, ALU.add, ALU.max)
                link(last)
                for h in range(HEADS):
                    last = nc.vector.tensor_tensor_scan(Q[:, ::-1, h], penn[:, ::-1], F[:, ::-1, h], 0.0, ALU.add, ALU.max)
                link(last)
                nc.vector.tensor_copy(ends[:, 0:HEADS], Q[:, 0, :])
                nc.vector.tensor_copy(ends[:, HEADS:2 * HEADS], Q[:, COLS - 1, :]).then_inc(s_ready, 1)
                dve.wait_ge(s_pe, 1)
                link(nc.vector.tensor_copy(keyr, ps[0][:, 0:256]))
                nc.vector.tensor_scalar(m_h, keyr, key0[:, 0:1], None, ALU.is_equal)
                link(nc.vector.tensor_scalar(m_t, keyr, key0[:, COLS - 1:COLS], None, ALU.is_equal))
                nc.vector.tensor_scalar(p_h, m_h, -1.0, BIG, ALU.add, ALU.mult)
                link(nc.vector.tensor_scalar(p_t, m_t, -1.0, BIG, ALU.add, ALU.mult))

                def combine(bank0, r, masks, op, op2):
                    dve.wait_ge(s_pe, r)
                    for s, m in enumerate(masks):
                        for half in range(2):
                            last = nc.vector.tensor_tensor(work[:, s, :, half * P:(half + 1) * P],
                                                           ps[bank0 + half][:, :].rearrange("p (h q) -> p h q", q=P),
                                                           m[:, half * P:(half + 1) * P].unsqueeze(1).to_broadcast([P, HEADS, P]), op)
                    link(last)
                    for s in range(2):
                        last = nc.vector.tensor_reduce(tot[:, s, :], work[:, s, :, :], AX_X, op2)
                    for h in range(HEADS):
                        last = nc.vector.tensor_tensor(M[:, :, h], Q[:, :, h], free_, ALU.mult)
                    link(last)
                    for s, m in ((0, hmask[:, :]), (1, tmask)):
                        for h in range(HEADS):
                            last = nc.vector.scalar_tensor_tensor(M[:, :, h], m, tot[:, s, h:h + 1], M[:, :, h], ALU.mult, ALU.add)
                        link(last)

                combine(3, 2, (p_h, p_t), ALU.add, ALU.max)
                nc.vector.tensor_tensor(Z[:, :, :], Z[:, :, :], M[:, :, :], ALU.subtract).then_inc(s_exp, 1)
                nc.vector.tensor_scalar(pm[:, 0:1], hmask[:, COLS - 1:COLS], -1.0, 1.0, ALU.mult, ALU.add)
                link(nc.vector.tensor_scalar(pen, nsame[:, :], -1.0, 1.0, ALU.mult, ALU.add))
                dve.wait_ge(s_exp, 2)
                for h in range(HEADS):
                    last = nc.vector.tensor_tensor_scan(F[:, :, h], same[:, :], Z[:, :, h], 0.0, ALU.mult, ALU.add)
                link(last)
                for h in range(HEADS):
                    last = nc.vector.tensor_tensor(F[:, :, h], F[:, :, h], pen, ALU.mult)
                link(last)
                for h in range(HEADS):
                    last = nc.vector.tensor_tensor_scan(Q[:, ::-1, h], nsame[:, ::-1], F[:, ::-1, h], 0.0, ALU.mult, ALU.add)
                link(last)
                nc.vector.tensor_copy(ends[:, 0:HEADS], Q[:, 0, :])
                nc.vector.tensor_scalar(ends[:, HEADS:2 * HEADS], Q[:, COLS - 1, :], pm[:, 0:1], None, ALU.mult).then_inc(s_ready, 1)
                combine(0, 3, (m_h, m_t), ALU.mult, ALU.add)
                link(nc.vector.reciprocal(M[:, :, :], M[:, :, :]))
                link(nc.vector.tensor_tensor(Z[:, :, :], Z[:, :, :], M[:, :, :], ALU.mult))

                nc.vector.memset(headrow, 0.0)
                link(nc.vector.scalar_tensor_tensor(carry_mask, keyr[:, 0:P], key0[:, COLS - 1:COLS], utri[:, :], ALU.is_equal, ALU.mult))

        ld_b = [sem("sc_base0"), sem("sc_base1")]
        sc_done = [sem("sc_done0"), sem("sc_done1")]
        (sc_rows, sc_run, sc_heads, sc_carry, sc_head_row, sc_chain, sc_bond, sc_ix, sc_go, sc_igo, sc_sig) = (sem("sc_" + n) for n in (
            "rows", "run", "heads", "carry", "head_row", "chain", "bond", "ix", "go", "igo", "sigmoid"))
        with nc.Block() as block:
            @block.sync
            def _(sp):
                def body(it, u, k):
                    if past(k):
                        sp.wait_ge(sc_rows, it - 1)
                    sp.dma_start(BS[:, u, :, :].rearrange("p c d -> p (c d)"), spill[:, bass.ds(it * G4 * D, G4 * D)]).then_inc(ld_b[u], 16)
                loop(sp, body)

            @block.vector
            def _(dve):
                dve.wait_ge(ld_bd, 16 * 4)
                STEPS = 6 + G4
                HEAD_SKIPPED = G4

                def head(it, u, c, v, mark, need):
                    if c == 0:
                        dve.wait_ge(sc_rows, it + 1)
                    else:
                        need(v)
                    return mark(nc.vector.scalar_tensor_tensor(headrow, O[:, u, c, :], hend[:, bass.ds(it * G4 + c, 1)], headrow,
                                                               ALU.mult, ALU.add))

                def body(it, u, k):
                    n = [0]

                    def mark(ins):
                        n[0] += 1
                        ins.then_inc(sc_chain, 1)
                        return STEPS * it + n[0] - (HEAD_SKIPPED if past(k) or u else 0)

                    def need(v):
                        dve.wait_ge(sc_chain, v)
                    hv = H[:, bass.ds(it * G4 * D, G4 * D)]
                    pv = Z[:, bass.ds(it * G4, G4), :].rearrange("p j h -> p (j h)").unsqueeze(2).to_broadcast([P, G4 * HEADS, HD])
                    h3 = hv.rearrange("p (g d) -> p g d", d=HD)
                    v = mark(nc.vector.tensor_tensor(h3, h3, pv, ALU.mult))
                    w = bwork[:, u, :, :]
                    b = mark(nc.vector.tensor_tensor(w, BD[:, bass.ds(it * G4 * BOND, G4 * BOND)].rearrange("p (j c) -> p j c", c=BOND),
                                                     wabr[:, :].unsqueeze(1).to_broadcast([P, G4, BOND]), ALU.mult))
                    vh = None
                    for c in range(G4):
                        j = it * G4 + c
                        if past(k) or u:
                            vh = head(it - 1, 1 - u, c, vh, mark, need)
                        before = col(j if isinstance(it, int) and j == 0 else j - 1)
                        need(v)
                        v = mark(nc.vector.scalar_tensor_tensor(H[:, col(j)], H[:, before], same[:, bass.ds(j, 1)], H[:, col(j)],
                                                                ALU.mult, ALU.add))
                        if c == 1:
                            need(b)
                            nc.vector.tensor_reduce(zb[:, bass.ds(it * G4, G4)], w, AX_X, ALU.add).then_inc(sc_bond, 1)
                    if past(k):
                        dve.wait_ge(sc_done[u], 16 * G4 * k)
                    dve.wait_ge(ld_b[u], 16 * (k + 1))
                    need(v)
                    if vh is not None:
                        need(vh)
                    if isinstance(it, int) and it == ITS - 1:
                        nc.vector.tensor_copy(tick, headrow[:, 0:1]).then_inc(sc_run, 1)
                    nc.vector.tensor_tensor(O[:, u, 0:G4, :], hv.rearrange("p (c d) -> p c d", d=D), BS[:, u, :, :], ALU.add).then_inc(sc_rows, 1)
                loop(dve, body)
                vh = None
                n = [STEPS * ITS]

                def mark(ins):
                    n[0] += 1
                    ins.then_inc(sc_chain, 1)
                    return n[0] - HEAD_SKIPPED

                def need(v):
                    dve.wait_ge(sc_chain, v)
                for c in range(G4):
                    vh = head(ITS - 1, 0, c, vh, mark, need)
                need(vh)
                dve.wait_ge(sc_carry, 1)
                nc.vector.tensor_tensor(O[:, 0, ROWS - 1, :], headrow, ps[6][:, 0:D], ALU.add).then_inc(sc_head_row, 1)

            @block.tensor
            def _(pe):
                pe.wait_ge(sc_run, 1)
                nc.tensor.matmul(ps[6][:, 0:D], carry_mask, H[:, (COLS - 1) * D:COLS * D], start=True, stop=True).then_inc(sc_carry, 1)

            @block.scalar
            def _(act):
                def body(it, u, k):
                    if past(k):
                        act.wait_ge(sc_done[u], 16 * G4 * k)
                    act.sem_inc(sc_igo, 1)
                    nc.scalar.copy(sx[:, u, :], sidx[:, bass.ds(it * G4, G4)]).then_inc(sc_ix, 1)
                loop(act, body)
                act.wait_ge(sc_bond, ITS)
                nc.scalar.activation(bw[:, :], zb, ACT.Sigmoid, bias=babr[:, 0:1]).then_inc(sc_sig, 1)
                act.wait_ge(sc_sig, 1)

            @block.gpsimd
            def _(pool):
                lim = pool.to_reg(N - 1)

                def body(it, u, k):
                    pool.wait_ge(sc_ix, it + 1)
                    pool.wait_ge(sc_rows, it + 1)
                    pool.sem_inc(sc_go, 1)
                    for c in range(G4):
                        pool.indirect_dma_start(x1, bass.IndirectOffsetOnAxis(sx[:, u, c:c + 1], 0), O[:, u, c, :], None,
                                                bounds_check=lim, oob_is_err=False).then_inc(sc_done[u], 16)
                loop(pool, body)
                pool.wait_ge(sc_head_row, 1)
                pool.indirect_dma_start(x1, bass.IndirectOffsetOnAxis(hidx[:, 0:1], 0), O[:, 0, ROWS - 1, :], None,
                                        bounds_check=lim, oob_is_err=False).then_inc(sc_heads, 16)
                pool.wait_ge(sc_heads, 16)
                for u in range(2):
                    pool.wait_ge(sc_done[u], 16 * G4 * (ITS // 2 + 1 - u))

        XN4 = [XN[:, 0, :, :], XN[:, 1, :, :]] + [XE[:, u, :, :, :].rearrange("p c s d -> p (c s) d") for u in range(2)]
        R4 = [R[:, 0:ROWS, :], R[:, ROWS:2 * ROWS, :], O[:, 0, :, :], O[:, 1, :, :]]
        XD4 = [BS[:, 0, :, :], BS[:, 1, :, :]] + [TS[:, u, :].rearrange("p (c d) -> p c d", d=D) for u in range(2)]
        ld_n = [sem(f"dn_nodes{u}") for u in range(4)]
        ld_d = [sem(f"dn_gathered{u}") for u in range(4)]
        st_n = [sem(f"dn_stored{u}") for u in range(4)]
        (dn_var, dn_std, dn_norm, dn_nodes, dn_kept, dn_out, dn_chain, dn_ix, dn_go, dn_kgo) = (
            sem("dn_" + n) for n in ("var", "std", "norm", "rows", "kept", "out", "chain", "ix", "go", "kept_go"))
        XS4 = [XE[:, u, 2 * v:2 * v + 2, :, :].rearrange("p c s d -> p (c s) d") for u in range(2) for v in range(2)]
        ld_s = [sem(f"ms_gathered{u}") for u in range(4)]
        ms_ix, ms_igo = sem("ms_ix"), sem("ms_igo")

        def loop4(eng, body):
            for it in range(4):
                body(it, it, 0)
            with eng.Fori(1, ITS // 4 - 1) as i:
                for u in range(4):
                    body(4 * i + u, u, i)
            for it in range(4 * (ITS // 4 - 1), ITS):
                body(it, it % 4, it // 4)

        with nc.Block() as block:
            @block.sync
            def _(sp):
                def load(it, u):
                    sp.dma_start(XN4[u], x1[bass.ds(node0(it), NODES_PER_IT), :].rearrange("(p r) c -> p r c", r=ROWS)).then_inc(ld_n[u], 16)

                def body(it, u, k):
                    sp.wait_ge(dn_out, it + 1)
                    if isinstance(it, int) and it == ITS - 1:
                        sp.wait_ge(st_n[(u + 3) % 4], 16 * (ITS // 4))
                    sp.dma_start(out[bass.ds(node0(it), NODES_PER_IT), :].rearrange("(p r) c -> p r c", r=ROWS), R4[u]).then_inc(st_n[u], 16)
                    if upto(it, ITS - 5):
                        load(it + 4, u)
                for n in range(4):
                    load(n, n)
                loop4(sp, body)
                for u in range(4):
                    sp.wait_ge(st_n[u], 16 * (ITS // 4 + (u == 0)))

            @block.gpsimd
            def _(pool):
                lim = pool.to_reg(N - 1)

                def gather(it, u):
                    pool.wait_ge(dn_ix, it + 1)
                    pool.sem_inc(dn_go, 1)
                    for c in range(G4):
                        pool.indirect_dma_start(XD4[u][:, c, :], None, x1, bass.IndirectOffsetOnAxis(ix[:, u, c:c + 1], 0),
                                                bounds_check=lim, oob_is_err=False).then_inc(ld_d[u], 16)

                def body(it, u, k):
                    if upto(it, ITS - 5):
                        pool.wait_ge(dn_kept, it + 1)
                        gather(it + 4, u)
                for n in range(4):
                    gather(n, n)
                loop4(pool, body)
                for n in range(4):
                    nc.gpsimd.tensor_copy(ixs[:, n, :], gidx[:, n * G4:(n + 1) * G4, 0]).then_inc(ms_ix, 1)
                    pool.wait_ge(ms_ix, n + 1)
                    if n % 2 == 0:
                        pool.wait_ge(dn_out, ITS - 2 + n // 2)
                    for c in range(G4):
                        pool.indirect_dma_start(XS4[n][:, c, :], None, x1, bass.IndirectOffsetOnAxis(ixs[:, n, c:c + 1], 0),
                                                bounds_check=lim, oob_is_err=False).then_inc(ld_s[n], 16)

            @block.vector
            def _(dve):
                def linker(base):
                    n = [0]

                    def link(ins):
                        n[0] += 1
                        ins.then_inc(dn_chain, 1)
                        dve.wait_ge(dn_chain, base + n[0])
                    return link

                def measure(it, u, k, par, link):
                    dve.wait_ge(ld_n[u], 16 * (k + 1))
                    for r in range(ROWS):
                        last = stats(XN4[u][:, r, :], r)
                    link(last)
                    moments(link, par, ROWS, dn_var)

                def finish(it, u):
                    dve.wait_ge(dn_nodes, it + 1)
                    nc.vector.scalar_tensor_tensor(R4[u], R4[u], 0.0, XN4[u], ALU.max, ALU.add).then_inc(dn_out, 1)

                def body(it, u, k):
                    par = u % 2
                    link = linker(4 * it + 4)
                    if upto(it, ITS - 2):
                        measure(it + 1, (u + 1) % 4, k + (u == 3), 1 - par, link)
                    if past(k) or u:
                        finish(it - 1, (u + 3) % 4)
                    if upto(it, ITS - 2):
                        dve.wait_ge(dn_std, it + 2)
                        scales(link, 1 - par, ROWS, dn_norm)
                        dve.wait_ge(dn_norm, it + 2)
                link = linker(0)
                measure(0, 0, 0, 0, link)
                dve.wait_ge(dn_std, 1)
                scales(link, 0, ROWS, dn_norm)
                dve.wait_ge(dn_norm, 1)
                loop4(dve, body)
                finish(ITS - 1, 0)

            @block.scalar
            def _(act):
                def indices(it, u):
                    nc.scalar.copy(ix[:, u, :], gidx[:, bass.ds(it * G4, G4), 1]).then_inc(dn_ix, 1)

                def keep(it, u, k):
                    act.wait_ge(ld_d[u], 16 * G4 * (k + 1))
                    act.sem_inc(dn_kgo, 1)
                    nc.scalar.copy(H[:, bass.ds(it * G4 * D, G4 * D)], XD4[u].rearrange("p c d -> p (c d)")).then_inc(dn_kept, 1)
                    if upto(it, ITS - 5):
                        indices(it + 4, u)

                def body(it, u, k):
                    par = u % 2
                    act.wait_ge(dn_norm, it + 1)
                    if past(k):
                        act.wait_ge(st_n[u], 16 * k)
                    for r in range(ROWS):
                        last = nc.scalar.activation(R4[u][:, r, :], XN4[u][:, r, :], ACT.Identity, bias=nmr[:, par, r:r + 1],
                                                    scale=rstd[:, par, r:r + 1])
                        if r == 5 and upto(it, ITS - 2):
                            act.wait_ge(dn_var, it + 2)
                            root(1 - par, ROWS, dn_std)
                    last.then_inc(dn_nodes, 1)
                    keep(it, u, k)
                for n in range(4):
                    indices(n, n)
                act.wait_ge(dn_var, 1)
                root(0, ROWS, dn_std)
                loop4(act, body)

        Nf4 = XN[:, :, :, :].rearrange("p u r d -> p (u r d)")
        HS, BT, HID, MS = (Nf4[:, n * 512:(n + 1) * 512] for n in range(4))
        S2 = [O[:, u, :, :].rearrange("p r d -> p (r d)") for u in range(2)]
        UPD = [BS[:, u, :, :].rearrange("p c d -> p (c d)") for u in range(2)] + [TS[:, u, :] for u in range(2)]
        junk = Rw[:, 0:768]
        cnt, tt, kcol, kdif = (Rw[:, 768 + 4 * n:772 + 4 * n] for n in range(4))
        bnd = Rw[:, 1024:1024 + G4 * BOND]
        (ms_var, ms_std, ms_norm, ms_src, ms_keys, ms_bond, ms_flip, ms_hs, ms_bt, ms_s, ms_cnt, ms_hid, ms_hidr, ms_msg,
         ms_scaled, ms_sum, ms_upd, ms_go, ms_sgo, ms_sx, ms_chain, ms_col) = (sem("ms_" + n) for n in (
            "var", "std", "norm", "src", "keys", "bond", "flip", "hs", "bt", "s", "cnt", "hid", "hidr", "msg",
            "scaled", "sum", "upd", "go", "sgo", "sx", "chain", "col"))
        ms_add = sem("ms_add")
        bK, (bB, bS, bH, bM, bU, bD) = ps[0:2], ps[2:8]
        XD = Z[:, :, :].rearrange("p j h -> p (j h)")[:, 0:G4 * D]
        HDST = Rw[:, 1280:1280 + G4 * D]
        ms_dst_v, ms_dst_a, ms_hd, ms_flipd, ms_dgo = (sem("ms_" + n) for n in ("dst_dve", "dst_act", "hd", "flipped_dst", "dst_go"))
        NM = 2 * G4
        DVE_DST = 2

        def hcol(it, c):
            return bass.ds(it * G4 * D + c * D, D)

        with nc.Block() as block:
            @block.gpsimd
            def _(pool):
                lim = pool.to_reg(N - 1)
                limo = pool.to_reg(N + 3 * P - 1)

                def fetch_ix(it, u):
                    pool.wait_ge(ms_ix, it + 1)
                    pool.sem_inc(ms_go, 1)

                def fetch(u, c):
                    pool.indirect_dma_start(XS4[u][:, c, :], None, x1, bass.IndirectOffsetOnAxis(ixs[:, u, c:c + 1], 0),
                                            bounds_check=lim, oob_is_err=False).then_inc(ld_s[u], 16)

                def body(it, u, k):
                    more = upto(it, ITS - 6)
                    for pair in range(2):
                        if pair == 0:
                            pool.wait_ge(ms_sx, it + 1)
                            pool.wait_ge(ms_upd, it + 1)
                        if past(k) or u or pair:
                            pool.wait_ge(ms_add, 32 * (2 * it + pair))
                        pool.sem_inc(ms_sgo, 1)
                        for c in (2 * pair, 2 * pair + 1):
                            pool.indirect_dma_start(out, bass.IndirectOffsetOnAxis(sx[:, u, c:c + 1], 0),
                                                    UPD[u][:, c * D:(c + 1) * D], None,
                                                    bounds_check=limo, oob_is_err=True, compute_op=ALU.add).then_inc(ms_add, 16)
                        if more:
                            if pair == 0:
                                pool.wait_ge(ms_flip, it + 2)
                                fetch_ix(it + 5, (u + 1) % 4)
                            fetch((u + 1) % 4, 2 * pair)
                            fetch((u + 1) % 4, 2 * pair + 1)
                pool.wait_ge(ms_flip, 1)
                fetch_ix(4, 0)
                for c in range(G4):
                    fetch(0, c)
                loop4(pool, body)
                pool.wait_ge(ms_add, 16 * COLS)

            @block.vector
            def _(dve):
                LINKS = 7

                def linker(base):
                    n = [0]

                    def link(ins):
                        n[0] += 1
                        ins.then_inc(ms_chain, 1)
                        dve.wait_ge(ms_chain, base + n[0])
                    return link

                def measure(it, u, k, par, link):
                    dve.wait_ge(ld_s[u], 16 * G4 * (k + 1))
                    for c in range(G4):
                        stats(XS4[u][:, c, :], c)
                    for c in range(G4):
                        last = stats(H[:, hcol(it, c)], G4 + c)
                    link(last)
                    moments(link, par, NM, ms_var)

                def rescale(it, par, link):
                    dve.wait_ge(ms_std, it + 1)
                    scales(link, par, NM, ms_norm)
                    dve.wait_ge(ms_norm, it + 1)
                    if past(it):
                        dve.wait_ge(ms_flipd, it)
                    for c in range(DVE_DST):
                        t = G4 + c
                        last = nc.vector.tensor_scalar(XD[:, c * D:(c + 1) * D], H[:, hcol(it, c)], rstd[:, par, t:t + 1],
                                                       nmr[:, par, t:t + 1], ALU.mult, ALU.add)
                    last.then_inc(ms_dst_v, 1)

                def match(it, u, early, reused, link):
                    dve.wait_ge(ms_keys, it + 1)
                    if not early:
                        dve.wait_ge(ms_sum, it - 1)
                    for c in range(G4):
                        kc = key1[:, bass.ds(it * G4 + c, 1)]
                        p0 = c // 2 * 2 * P
                        nc.vector.tensor_scalar(S2[u % 2][:, c * 2 * P:(c + 1) * 2 * P], bK[u % 2][:, p0:p0 + 2 * P], kc, None, ALU.is_equal)
                        w = (1 + c % 2) * P
                        j0 = c // 2 * 3 * P + c % 2 * P
                        nc.vector.scalar_tensor_tensor(junk[:, j0:j0 + w], bK[u % 2][:, p0:p0 + w], kc, ltri[:, 2 * P - w:2 * P],
                                                       ALU.is_equal, ALU.mult, accum_out=cnt[:, c:c + 1])
                    k4 = key1[:, bass.ds(it * G4, G4)]
                    link(nc.vector.tensor_tensor(kdif, spare[:, :], k4, ALU.subtract))
                    link(nc.vector.tensor_scalar(tt, cnt, 1.0, None, ALU.min))
                    link(nc.vector.tensor_tensor(tt, kdif, tt, ALU.mult))
                    if reused:
                        dve.wait_ge(ms_add, 16 * G4 * (it - 3))
                    nc.vector.tensor_tensor(sx[:, u, :], tt, k4, ALU.add).then_inc(ms_sx, 1)

                def body(it, u, k):
                    late = max(0, it - (ITS - 3)) if isinstance(it, int) else 0
                    link = linker(LINKS * it + 15 - 4 * late)
                    dve.wait_ge(ms_msg, it + 1)
                    for c in range(G4):
                        last = nc.vector.tensor_scalar(MS[:, c * D:(c + 1) * D], bM[:, c * D:(c + 1) * D], bw[:, bass.ds(it * G4 + c, 1)],
                                                       None, ALU.mult)
                    last.then_inc(ms_scaled, 1)
                    if upto(it, ITS - 4):
                        measure(it + 3, (u + 3) % 4, k + (u >= 1), (u + 1) % 2, link)
                    if upto(it, ITS - 2):
                        match(it + 1, (u + 1) % 4, not (past(k) or u), past(k) or u == 3, link)
                    if upto(it, ITS - 4):
                        rescale(it + 3, (u + 1) % 2, link)
                link = linker(0)
                for n in range(3):
                    measure(n, n, 0, n % 2, link)
                    rescale(n, n % 2, link)
                    if n == 0:
                        match(0, 0, True, False, link)
                loop4(dve, body)

            @block.scalar
            def _(act):
                def indices(it, u):
                    act.sem_inc(ms_igo, 1)
                    nc.scalar.copy(ixs[:, u, :], gidx[:, bass.ds(it * G4, G4), 0]).then_inc(ms_ix, 1)

                def columns(it):
                    nc.scalar.copy(bnd, BD[:, bass.ds(it * G4 * BOND, G4 * BOND)])
                    nc.scalar.copy(kcol, key1[:, bass.ds(it * G4, G4)]).then_inc(ms_col, 1)

                def rescale(it, u, par):
                    act.wait_ge(ms_norm, it + 1)
                    for c in range(G4):
                        last = nc.scalar.activation(XS4[u][:, c, :], XS4[u][:, c, :], ACT.Identity, bias=nmr[:, par, c:c + 1],
                                                    scale=rstd[:, par, c:c + 1])
                    last.then_inc(ms_src, 1)
                    if past(it):
                        act.wait_ge(ms_flipd, it)
                    act.sem_inc(ms_dgo, 1)
                    for c in range(DVE_DST, G4):
                        t = G4 + c
                        last = nc.scalar.activation(XD[:, c * D:(c + 1) * D], H[:, hcol(it, c)], ACT.Identity, bias=nmr[:, par, t:t + 1],
                                                    scale=rstd[:, par, t:t + 1])
                    last.then_inc(ms_dst_a, 1)

                def take_bond(it):
                    act.wait_ge(ms_bond, it + 1)
                    if past(it):
                        act.wait_ge(ms_hid, it)
                    nc.scalar.copy(BT[0:BOND, :], bB[0:BOND, :]).then_inc(ms_bt, 1)

                def take_src(it):
                    act.wait_ge(ms_flip, it + 1)
                    if past(it):
                        act.wait_ge(ms_hid, it)
                    nc.scalar.activation(HS, bS[:, :], ACT.Relu).then_inc(ms_hs, 1)

                def take_dst(it):
                    act.wait_ge(ms_flipd, it + 1)
                    if past(it):
                        act.wait_ge(ms_hid, it)
                    nc.scalar.activation(HDST, bD[:, :], ACT.Relu).then_inc(ms_hd, 1)

                def take_hidden(it):
                    act.wait_ge(ms_hid, it + 1)
                    if past(it):
                        act.wait_ge(ms_msg, it)
                    nc.scalar.activation(HID, bH[:, :], ACT.Relu, bias=b1c[:, 0:1]).then_inc(ms_hidr, 1)

                def body(it, u, k):
                    if upto(it, ITS - 2):
                        take_hidden(it + 1)
                    if upto(it, ITS - 4):
                        act.wait_ge(ms_var, it + 4)
                        root((u + 1) % 2, NM, ms_std)
                    if upto(it, ITS - 6):
                        indices(it + 5, (u + 1) % 4)
                    act.wait_ge(ms_sum, it + 1)
                    if past(k):
                        act.wait_ge(ms_add, 16 * G4 * (it - 3))
                    nc.scalar.copy(UPD[u], bU[:, :]).then_inc(ms_upd, 1)
                    if upto(it, ITS - 3):
                        take_dst(it + 2)
                        take_src(it + 2)
                        take_bond(it + 2)
                    if upto(it, ITS - 4):
                        columns(it + 3)
                        rescale(it + 3, (u + 3) % 4, (u + 1) % 2)

                columns(0)
                for n in range(3):
                    act.wait_ge(ms_var, n + 1)
                    root(n % 2, NM, ms_std)
                    rescale(n, n, n % 2)
                    if n < 2:
                        take_dst(n)
                        take_src(n)
                        take_bond(n)
                        columns(n + 1)
                    if n == 0:
                        indices(4, 0)
                        take_hidden(0)
                loop4(act, body)

            @block.tensor
            def _(pe):
                def keys(it, u):
                    pe.wait_ge(ms_col, it + 1)
                    if past(it):
                        pe.wait_ge(ms_bt, it)
                    if not isinstance(it, int) or it > 1:
                        pe.wait_ge(ms_sx, it - 1)
                    for c in range(G4):
                        last = nc.tensor.transpose(bK[u % 2][:, c * D:(c + 1) * D], kcol[:, c:c + 1].to_broadcast([P, P]), ident[:, :])
                    last.then_inc(ms_keys, 1)
                    for c in range(G4):
                        last = nc.tensor.transpose(bB[0:BOND, c * D:(c + 1) * D], bnd[:, c * BOND:(c + 1) * BOND], ident[:, :])
                    last.then_inc(ms_bond, 1)

                def flip(it, u):
                    pe.wait_ge(ms_src, it + 1)
                    if past(it):
                        pe.wait_ge(ms_hs, it)
                    for c in range(G4):
                        last = nc.tensor.transpose(bS[:, c * D:(c + 1) * D], XS4[u % 4][:, c, :], ident[:, :])
                    last.then_inc(ms_flip, 1)

                def flip_dst(it):
                    pe.wait_ge(ms_dst_v, it + 1)
                    pe.wait_ge(ms_dst_a, it + 1)
                    if past(it):
                        pe.wait_ge(ms_hd, it)
                    for c in range(G4):
                        last = nc.tensor.transpose(bD[:, c * D:(c + 1) * D], XD[:, c * D:(c + 1) * D], ident[:, :])
                    last.then_inc(ms_flipd, 1)

                def hidden(it):
                    if past(it):
                        pe.wait_ge(ms_hidr, it)
                    pe.wait_ge(ms_hd, it + 1)
                    nc.tensor.matmul(bH[:, :], w1s[:, 1, :], HDST, start=True, stop=False)
                    pe.wait_ge(ms_bt, it + 1)
                    nc.tensor.matmul(bH[:, :], w1s[0:BOND, 2, :], BT[0:BOND, :], start=False, stop=False)
                    pe.wait_ge(ms_hs, it + 1)
                    nc.tensor.matmul(bH[:, :], w1s[:, 0, :], HS, start=False, stop=True).then_inc(ms_hid, 1)

                def messages(it):
                    if past(it):
                        pe.wait_ge(ms_scaled, it)
                    nc.tensor.matmul(bM[:, :], on3[:, :], b3[:, 1, :], start=True, stop=False, skip_group_check=True)
                    pe.wait_ge(ms_hidr, it + 1)
                    for c in range(G4):
                        last = nc.tensor.matmul(bM[:, c * D:(c + 1) * D], HID[:, c * D:(c + 1) * D], w2s[:, :],
                                                start=False, stop=(c == G4 - 1), skip_group_check=True)
                    last.then_inc(ms_msg, 1)

                def body(it, u, k):
                    if upto(it, ITS - 2):
                        hidden(it + 1)
                    pe.wait_ge(ms_scaled, it + 1)
                    if past(k) or u:
                        pe.wait_ge(ms_upd, it)
                    pe.wait_ge(ms_sx, it + 1)
                    for c in range(G4):
                        for b in (c // 2 * 2, c // 2 * 2 + 1):
                            last = nc.tensor.matmul(bU[:, c * D:(c + 1) * D], S2[u % 2][:, (2 * b + c % 2) * P:(2 * b + c % 2 + 1) * P],
                                                    MS[:, b * D:(b + 1) * D], start=(b % 2 == 0), stop=(b % 2 == 1), skip_group_check=True)
                    last.then_inc(ms_sum, 1)
                    if upto(it, ITS - 3):
                        flip_dst(it + 2)
                        flip(it + 2, u + 2)
                        keys(it + 2, u)
                    if upto(it, ITS - 2):
                        messages(it + 1)
                keys(0, 0)
                flip_dst(0)
                flip(0, 0)
                hidden(0)
                messages(0)
                flip_dst(1)
                flip(1, 1)
                keys(1, 1)
                loop4(pe, body)


_INS = ['x', 'src', 'dst', 'edge_attr_64', 'L0_gnn_W_embed', 'L0_gnn_a_src', 'L0_gnn_a_dst', 'L0_gnn_W_lin', 'L0_gnn_bias',
        'L1_gnn_W1', 'L1_gnn_b1', 'L1_gnn_W2', 'L1_gnn_b2', 'L1_gnn_Wa', 'L1_gnn_ba']


def kernel(**inputs):
    import numpy as _np
    import concourse.bacc as _bacc
    from concourse import mybir as _mybir
    from concourse.bass_utils import run_bass_kernel_spmd as _run

    nc = _bacc.Bacc("TRN2", target_bir_lowering=False, num_devices=1)
    arrays, args = {}, []
    for name in _INS:
        a = _np.ascontiguousarray(inputs[name])
        arrays[f"in_{name}_dram"] = a
        args.append(nc.dram_tensor(f"in_{name}_dram", a.shape, _mybir.dt.from_np(a.dtype), kind="ExternalInput").ap())
    n = inputs["x"].shape[0]
    args.append(nc.dram_tensor("out_0_dram", (n + 384, 128), _mybir.dt.float32, kind="ExternalOutput").ap())
    gnn_program(nc, *args)
    r = _run(nc, [arrays], core_ids=[0])
    return r.results[0]["out_0_dram"][:n]
```
